# Optimizing a Trainium2 kernel written in Bass

```python
import numpy as np
import jax
import jax.numpy as jnp

def _softmax(x, axis=-1):
    return jax.nn.softmax(x, axis=axis)

def _gelu(x):
    return jax.nn.gelu(x, approximate=True)

def _silu(x):
    return jax.nn.silu(x)

def _sigmoid(x):
    return jax.nn.sigmoid(x)

def _layernorm(x, axis=-1, eps=1e-05):
    m = jnp.mean(x, axis=axis, keepdims=True)
    v = jnp.var(x, axis=axis, keepdims=True)
    return (x - m) / jnp.sqrt(v + eps)

def _scatter_add(tgt, idx, src, axis=0):
    return tgt.at[idx].add(src)

def _segment_sum(src, seg, n):
    return jax.ops.segment_sum(src, seg, n)
kernel_name = 'mk_gnn_preln_d2_gnn_r8_cfbc55'

def setup_inputs(seed: int=0):
    np.random.seed(seed)
    _w = jnp.asarray

    def _rec_inputs():
        import jax
        import jax.numpy as jnp
        _gk = jax.random.key(seed)
        x = -0.0009044 + 1 * jax.random.normal(jax.random.fold_in(_gk, 1), (12500, 16), jnp.float32)
        src = jax.random.randint(jax.random.fold_in(_gk, 2), (400000,), 0, 12500, jnp.int32)
        dst = jax.random.randint(jax.random.fold_in(_gk, 3), (400000,), 0, 12500, jnp.int32)
        _o = jnp.argsort(dst, stable=True)
        src = src[_o]
        dst = dst[_o]
        edge_attr_16 = 2.32446e-05 + 1 * jax.random.normal(jax.random.fold_in(_gk, 12), (400000, 16), jnp.float32)
        edge_attr_2 = 0.000411684 + 0.577418 * jax.random.normal(jax.random.fold_in(_gk, 13), (400000, 2), jnp.float32)
        return (x, src, dst, edge_attr_16, edge_attr_2)
    x, src, dst, edge_attr_16, edge_attr_2 = _rec_inputs()

    def _L0_gnn_setup():
        import jax, jax.numpy as jnp
        import numpy as np
        N_NODES = 12500
        N_EDGES = 200000
        F_IN = 16
        F_OUT = 16
        N_BASIS = 4

        def linear_basis(u, n):
            centers = jnp.linspace(-1.0, 1.0, n, dtype=u.dtype)
            dx = 2.0 / (n - 1)
            return jnp.maximum(0.0, 1.0 - jnp.abs(u[:, None] - centers[None, :]) / dx)
        key = jax.random.key(seed)
        k1, k2, k3, k4, k5 = jax.random.split(key, 5)
        x = jax.random.normal(k1, (N_NODES, F_IN), dtype=jnp.float32)
        edge_index = jax.random.randint(k2, (2, N_EDGES), 0, N_NODES, dtype=jnp.int64)
        edge_attr = jax.random.uniform(k3, (N_EDGES, 2), dtype=jnp.float32, minval=-1.0, maxval=1.0)
        weight = jax.random.uniform(k4, (N_BASIS, N_BASIS, F_IN, F_OUT), dtype=jnp.float32, minval=-0.05, maxval=0.05)
        return {'x': x, 'edge_index': edge_index, 'edge_attr': edge_attr, 'weight': weight}
    _L0_gnn_all = _L0_gnn_setup()
    _L0_gnn_in = {k: v for k, v in _L0_gnn_all.items() if k in ('weight',)}
    del _L0_gnn_all

    def _L1_gnn_setup():
        import jax, jax.numpy as jnp
        import numpy as np
        N_NODES = 6250
        N_EDGES = 62500
        IN_F = 16
        OUT_F = 16
        E_DIM = 16
        key = jax.random.key(seed)
        k1, k2, k3, k4, k5 = jax.random.split(key, 5)
        feat = jax.random.normal(k1, (N_NODES, IN_F), dtype=jnp.float32)
        efeat = jax.random.normal(k2, (N_EDGES, E_DIM), dtype=jnp.float32)
        W_e = jax.random.normal(k3, (E_DIM, IN_F * OUT_F), dtype=jnp.float32) * (1.0 / np.sqrt(E_DIM))
        b_e = jnp.zeros((IN_F * OUT_F,), dtype=jnp.float32)
        bias = jnp.zeros((OUT_F,), dtype=jnp.float32)
        src = jax.random.randint(k4, (N_EDGES,), 0, N_NODES, dtype=jnp.int32)
        dst = jax.random.randint(k5, (N_EDGES,), 0, N_NODES, dtype=jnp.int32)
        return {'feat': feat, 'efeat': efeat, 'W_e': W_e, 'b_e': b_e, 'bias': bias, 'src': src, 'dst': dst}
    _L1_gnn_all = _L1_gnn_setup()
    _L1_gnn_in = {k: v for k, v in _L1_gnn_all.items() if k in ('W_e', 'b_e', 'bias')}
    del _L1_gnn_all
    return {'x': x, 'src': src, 'dst': dst, 'edge_attr_16': edge_attr_16, 'edge_attr_2': edge_attr_2, 'L0_gnn_weight': _L0_gnn_in['weight'], 'L1_gnn_W_e': _L1_gnn_in['W_e'], 'L1_gnn_b_e': _L1_gnn_in['b_e'], 'L1_gnn_bias': _L1_gnn_in['bias']}

def reference(x, src, dst, edge_attr_16, edge_attr_2, L0_gnn_weight, L1_gnn_W_e, L1_gnn_b_e, L1_gnn_bias):
    import jax
    import jax.numpy as jnp

    def _L0_gnn_ref(x, edge_index, edge_attr, weight):
        import jax, jax.numpy as jnp
        import numpy as np
        N_NODES = 12500
        N_EDGES = 200000
        F_IN = 16
        F_OUT = 16
        N_BASIS = 4

        def linear_basis(u, n):
            centers = jnp.linspace(-1.0, 1.0, n, dtype=u.dtype)
            dx = 2.0 / (n - 1)
            return jnp.maximum(0.0, 1.0 - jnp.abs(u[:, None] - centers[None, :]) / dx)
        "BasisConvLayer forward, mode='conv', linear basis, no bias/activations.\n\n            For each edge e=(i<-j): msg_e = sum_{u,v} b_u(dx) b_v(dy) * (x_j @ W[u,v]);\n            out[i] = sum over incoming edges of msg_e.\n            "
        row, col = (edge_index[0], edge_index[1])
        x_j = x[col]
        bx = linear_basis(edge_attr[:, 0], N_BASIS)
        by = linear_basis(edge_attr[:, 1], N_BASIS)
        t = (bx[:, :, None] * by[:, None, :]).reshape(-1, N_BASIS * N_BASIS)
        w_flat = weight.reshape(N_BASIS * N_BASIS, F_IN, F_OUT)
        msg = jnp.zeros((x_j.shape[0], F_OUT), dtype=x.dtype)
        for k in range(N_BASIS * N_BASIS):
            msg = msg + t[:, k, None] * (x_j @ w_flat[k])
        out = jax.ops.segment_sum(msg, row, num_segments=N_NODES)
        return out

    def _L1_gnn_ref(feat, efeat, W_e, b_e, bias, src, dst):
        import jax, jax.numpy as jnp
        import numpy as np
        N_NODES = 6250
        N_EDGES = 62500
        IN_F = 16
        OUT_F = 16
        E_DIM = 16
        E = efeat.shape[0]
        N, in_f = feat.shape
        out_f = bias.shape[0]
        ew = (efeat @ W_e + b_e).reshape(E, in_f, out_f)
        msg = jnp.einsum('ei,eio->eo', feat[src], ew)
        summed = jax.ops.segment_sum(msg, dst, num_segments=N)
        cnt = jax.ops.segment_sum(jnp.ones((E,), feat.dtype), dst, num_segments=N)
        neigh = summed / jnp.maximum(cnt, 1.0)[:, None]
        return neigh + bias
    edge_index = jnp.stack([src, dst])
    h = jnp.maximum(_layernorm(x, axis=-1), 0.0)
    x = x + _L0_gnn_ref(h, edge_index, edge_attr_2, L0_gnn_weight)
    h = jnp.maximum(_layernorm(x, axis=-1), 0.0)
    x = x + _L1_gnn_ref(h, edge_attr_16, L1_gnn_W_e, L1_gnn_b_e, L1_gnn_bias, src, dst)
    return x

_drawn_inputs = setup_inputs


def setup_inputs(seed=0):
    import zlib

    import numpy as np

    out = dict(_drawn_inputs(seed))
    spreads = {'L1_gnn_b_e': (0.0, 0.1), 'L1_gnn_bias': (0.0, 0.1)}
    factors = {}
    for name, (base, spread) in spreads.items():
        noise = np.random.default_rng([zlib.crc32(name.encode()), seed]).standard_normal(out[name].shape)
        drawn = base * np.exp(spread * noise) if base else spread * noise
        out[name] = jnp.asarray(drawn.astype(out[name].dtype))
    for name, factor in factors.items():
        out[name] = (out[name] * factor).astype(out[name].dtype)
    return out
```

```python
from contextlib import ExitStack

import concourse.bass as bass
import numpy as np
from concourse import mybir

P = 128
N_NODES, N_EDGES, F = 12500, 400000, 16
LO = P // F
BLOCKS = -(-N_NODES // (P * LO))
PADDED = BLOCKS * P * LO
WHOLE = N_NODES // (P * LO)
TAIL_P = (N_NODES - WHOLE * P * LO) // LO
TAIL_LO = N_NODES - WHOLE * P * LO - TAIL_P * LO
HI = -(-N_NODES // LO)
BANKS = 4
HC = -(-HI // BANKS)
TILES = N_EDGES // P
GT = 5
SLOTS = 5
TURN = GT * SLOTS
TURNS = TILES // TURN
K = 16
NB = 4
PARTS = 3
KF = K * F
ROW = [KF, KF + F]
EPS = 1e-5
PQ = BLOCKS * LO
FREE = 1


def build(nc, x_in, src_in, dst_in, ea16_in, ea2_in, w0_in, we_in, be_in, bias_in, out):
    fp32, bf16, fp16, i32 = mybir.dt.float32, mybir.dt.bfloat16, mybir.dt.float16, mybir.dt.int32
    ALU, ACT, AX = mybir.AluOpType, mybir.ActivationFunctionType, mybir.AxisListType
    ds = bass.ds

    ctx = ExitStack()
    with ctx:
        def sb(name, shape, dt):
            return ctx.enter_context(nc.sbuf_tensor(name, shape, dt))

        def pb(name, shape, dt):
            return ctx.enter_context(nc.psum_tensor(name, shape, dt))

        def sem(name):
            return ctx.enter_context(nc.semaphore(name))

        table = [nc.dram_tensor(f"table{l}", (PADDED, ROW[l]), fp32, kind="Internal").ap() for l in (0, 1)]

        xs = sb("xs", [P, BLOCKS, P], fp32)
        hs = sb("hs", [P, BLOCKS, P], fp32)
        sq = sb("sq", [P, BLOCKS, P], fp32)
        stat = sb("stat", [P, 3, PQ], fp32)
        ends = [sb("dst_ids", [P, TILES], i32), sb("src_ids", [P, TILES], i32)]
        ea2 = sb("ea2", [P, TILES * 2], fp32)
        ident = sb("ident", [P, P], fp32)
        iota_hi = sb("iota_hi", [P, BANKS * HC], fp16)
        iota_lo = sb("iota_lo", [P, LO], fp32)
        iota_p = sb("iota_p", [P, P], fp32)
        iota_q = iota_p[:, 0:PQ]
        iota_row = sb("iota_row", [P, P], fp32)
        centers = sb("centers", [P, NB], fp32)
        zero = sb("zero", [P, HC], bf16)
        one = sb("one", [P, 1], fp32)
        bias_rows = sb("bias_rows", [P, F], fp32)
        w_nat = sb("w_nat", [F, 2, K, F], fp32)
        w_row = sb("w_row", [F, 2, ROW[1]], fp32)
        w_bd = [sb(f"w_bd{l}", [P, LO, ROW[l]], fp32) for l in (0, 1)]
        h_blk = sb("h_blk", [P, P], fp32)
        hT = sb("hT", [P, P], fp32)
        g_out = sb("g_out", [P, LO * ROW[1]], fp32)
        ids = sb("ids", [P, SLOTS, GT], i32)
        g = sb("g", [P, SLOTS, GT, ROW[1]], fp32)
        coef1 = sb("coef1", [P, SLOTS, GT, K], fp32)
        hats = sb("hats", [P, TURN, 2, NB], fp32)
        coef0 = sb("coef0", [P, TURN, K], fp32)
        prod = sb("prod", [P, GT, F, K], fp32)
        msg = sb("msg", [P, 2, GT, F], fp32)
        part = sb("part", [P, PARTS, GT, F], bf16)
        tgt_i = sb("tgt_i", [P, 4, TURN], i32)
        hi_f = sb("hi_f", [P, TURN], fp32)
        lo_f = sb("lo_f", [P, TURN], fp32)
        pq_f = sb("pq_f", [P, 2, TURN], fp32)
        oh_lo = sb("oh_lo", [P, TURN, LO], bf16)
        lhs = sb("lhs", [P, SLOTS, PARTS, GT, P], bf16)
        oh_hi = sb("oh_hi", [P, GT, BANKS, HC], bf16)
        sq_pq = sb("sq_pq", [P, GT, P + PQ], bf16)
        oh_pq = sb("oh_pq", [P, GT, P + PQ], bf16)
        acc_sb = sq[:, :, :].rearrange("p b c -> p (b c)")

        acc = pb("acc", [P, BANKS, 512], fp32)
        cnt = pb("cnt", [P, 512], fp32)
        ps_t = pb("ps_t", [P, 512], fp32)
        ps_g = pb("ps_g", [P, 2, 512], fp32)

        loads = sem("loads")
        w_loads, w_rows, bd_zero, bd_here = sem("w_loads"), sem("w_rows"), sem("bd_zero"), sem("bd_here")
        iota_made, ident_made, consts_made, tail_zero = (
            sem("iota_made"), sem("ident_made"), sem("consts_made"), sem("tail_zero"))
        dve_step = sem("dve_step")
        pool_step = sem("pool_step")
        act_step = sem("act_step")
        var_ready, sd_ready = sem("var_ready"), sem("sd_ready")
        h_ready = [sem(f"h_ready{l}") for l in (0, 1)]
        blk_ready = [sem(f"blk_ready{l}") for l in (0, 1)]
        blk_turned = [sem(f"blk_turned{l}") for l in (0, 1)]
        hT_ready = [sem(f"hT_ready{l}") for l in (0, 1)]
        g_made = [sem(f"g_made{l}") for l in (0, 1)]
        g_copied = [[sem(f"g_copied{l}_{b}") for b in (0, 1)] for l in (0, 1)]
        table_stored = [sem(f"table_stored{l}") for l in (0, 1)]
        ids_ready = [sem(f"ids_ready{l}") for l in (0, 1)]
        ids_settled = sem("ids_settled")
        rows_here = [[sem(f"rows_here{l}_{s}") for s in range(SLOTS)] for l in (0, 1)]
        rows_used = [[sem(f"rows_used{l}_{s}") for s in range(SLOTS)] for l in (0, 1)]
        coef_here = [sem(f"coef_here_{s}") for s in range(SLOTS)]
        pq_ready, pq_used = sem("pq_ready"), sem("pq_used")
        lhs_ready = [sem(f"lhs_ready{l}") for l in (0, 1)]
        hi_ready = [sem(f"hi_ready{l}") for l in (0, 1)]
        cnt_ready = sem("cnt_ready")
        tile_done = [[sem(f"tile_done{l}_{j}") for j in range(GT)] for l in (0, 1)]
        acc_done = [sem(f"acc_done{l}") for l in (0, 1)]
        acc_copied = [sem(f"acc_copied{l}") for l in (0, 1)]
        sums_turned = [sem(f"sums_turned{l}") for l in (0, 1)]
        sums_added = [sem(f"sums_added{l}") for l in (0, 1)]
        x_final, stored = sem("x_final"), sem("stored")
        N_LOADS = 7

        block = ctx.enter_context(nc.Block())

        @block.sync
        def _(sp):
            top = WHOLE * P * LO
            sp.wait_ge(tail_zero, 1)
            sp.dma_start(xs[:, 0:WHOLE, :], x_in[0:top, :].rearrange("(c p l) f -> p c (l f)", p=P, l=LO)).then_inc(loads, 16)
            sp.dma_start(xs[0:TAIL_P, WHOLE, :], x_in[top:top + TAIL_P * LO, :].rearrange("(p l) f -> p (l f)", l=LO)).then_inc(loads, 16)
            sp.dma_start(xs[TAIL_P:TAIL_P + 1, WHOLE, 0:TAIL_LO * F],
                         x_in[top + TAIL_P * LO:N_NODES, :].rearrange("(p l) f -> p (l f)", l=TAIL_LO)).then_inc(loads, 16)
            sp.dma_start(w_nat[:, 0, :, :], w0_in.rearrange("u v i o -> i (u v) o")).then_inc(w_loads, 16)
            sp.dma_start(w_nat[:, 1, :, :], we_in.rearrange("d (i o) -> i d o", o=F)).then_inc(w_loads, 16)
            sp.dma_start(w_row[:, 1, KF:KF + F], be_in.rearrange("(i o) -> i o", o=F)).then_inc(w_loads, 16)
            sp.dma_start(ends[0][:, :], dst_in.rearrange("(p t) -> p t", p=P)).then_inc(loads, 16)
            sp.dma_start(ends[1][:, :], src_in.rearrange("(p t) -> p t", p=P)).then_inc(loads, 16)
            sp.dma_start(ea2[:, :], ea2_in.rearrange("(p t) c -> p (t c)", p=P)).then_inc(loads, 16)
            sp.dma_start(bias_rows[:, :], bias_in.rearrange("(a o) -> a o", a=1).to_broadcast([P, F])).then_inc(loads, 16)
            sp.wait_ge(w_rows, 1)
            sp.wait_ge(bd_zero, 1)
            for l in (0, 1):
                for lo in range(LO):
                    sp.dma_start(w_bd[l][F * lo:F * lo + F, lo, :], w_row[:, l, 0:ROW[l]]).then_inc(bd_here, 16)
            for l in (0, 1):
                rows = table[l].rearrange("(c p l) r -> c p (l r)", p=P, l=LO)
                with sp.Fori(0, BLOCKS) as c:
                    for b in (0, 1):
                        sp.wait_ge(g_copied[l][b], (c + 1) * (LO // 2) + FREE)
                    sp.dma_start(rows[ds(c, 1), :, :].rearrange("a p r -> (a p) r"),
                                 g_out[:, 0:LO * ROW[l]]).then_inc(table_stored[l], 16)
                if l == 1:
                    ea = ea16_in.rearrange("(p t) d -> p (t d)", p=P)
                    with sp.Fori(0, TURNS) as i:
                        for s in range(SLOTS):
                            sp.wait_ge(rows_used[1][s], FREE + i)
                            sp.dma_start(coef1[:, s, :, :].rearrange("p t d -> p (t d)"),
                                         ea[:, ds(i * (TURN * K) + s * GT * K, GT * K)]).then_inc(coef_here[s], 16)
            sp.wait_ge(x_final, 1)
            sp.dma_start(out[0:top, :].rearrange("(c p l) f -> p c (l f)", p=P, l=LO), hs[:, 0:WHOLE, :]).then_inc(stored, 16)
            sp.dma_start(out[top:top + TAIL_P * LO, :].rearrange("(p l) f -> p (l f)", l=LO), hs[0:TAIL_P, WHOLE, :]).then_inc(stored, 16)
            sp.dma_start(out[top + TAIL_P * LO:N_NODES, :].rearrange("(p l) f -> p (l f)", l=TAIL_LO),
                         hs[TAIL_P:TAIL_P + 1, WHOLE, 0:TAIL_LO * F]).then_inc(stored, 16)
            sp.wait_ge(stored, 3 * 16)

        @block.gpsimd
        def _(pool):
            nc.gpsimd.iota(iota_p[:, :], [[1, P]], base=0, channel_multiplier=0, allow_small_or_imprecise_dtypes=True).then_inc(iota_made, 1)
            nc.gpsimd.iota(iota_row[:, :], [[0, P]], base=0, channel_multiplier=1, allow_small_or_imprecise_dtypes=True).then_inc(iota_made, 1)
            nc.gpsimd.iota(iota_lo[:, :], [[1, LO]], base=0, channel_multiplier=0, allow_small_or_imprecise_dtypes=True).then_inc(iota_made, 1)
            nc.gpsimd.iota(iota_hi[:, :], [[1, BANKS * HC]], base=0, channel_multiplier=0, allow_small_or_imprecise_dtypes=True).then_inc(iota_made, 1)
            pool.wait_ge(loads, 16 * N_LOADS)
            for l in (0, 1):
                pool.wait_ge(table_stored[l], 16 * (FREE + BLOCKS))
                with pool.Fori(0, TURNS) as i:
                    for s in range(SLOTS):
                        pool.wait_ge(rows_used[l][s], FREE + i)
                        nc.gpsimd.tensor_copy(ids[:, s, :], ends[l][:, ds(i * TURN + s * GT, GT)]).then_inc(ids_ready[l], 1)
                        pool.wait_ge(ids_ready[l], i * SLOTS + s + 1)
                        pool.sem_inc(ids_settled, 1)
                        for j in range(GT):
                            nc.gpsimd.indirect_dma_start(
                                out=g[:, s, j, 0:ROW[l]], out_offset=None, in_=table[l],
                                in_offset=bass.IndirectOffsetOnAxis(ap=ids[:, s, j:j + 1], axis=0),
                            ).then_inc(rows_here[l][s], 16)

        @block.scalar
        def _(act):
            for l in (0, 1):
                act.sem_inc(table_stored[l], 16 * FREE)
                act.sem_inc(hT_ready[l], FREE)
                for b in (0, 1):
                    act.sem_inc(g_copied[l][b], FREE)
                act.wait_ge(var_ready, l + 1)
                nc.scalar.activation(stat[:, 2, :], stat[:, 1, :], ACT.Sqrt).then_inc(sd_ready, 1)
                with act.Fori(0, BLOCKS) as c:
                    act.wait_ge(blk_turned[l], FREE + c + 1)
                    act.wait_ge(g_made[l], FREE + c * LO)
                    nc.scalar.copy(hT[:, :], ps_t[:, 0:P]).then_inc(hT_ready[l], 1)
                    act.wait_ge(table_stored[l], (FREE + c) * 16)
                    for lo in range(LO):
                        act.wait_ge(g_made[l], c * LO + (FREE + lo + 1))
                        nc.scalar.copy(g_out[:, lo * ROW[l]:(lo + 1) * ROW[l]],
                                       ps_g[:, lo % 2, 0:ROW[l]]).then_inc(g_copied[l][lo % 2], 1)
            act.sem_inc(pq_used, FREE)
            with act.Fori(0, TURNS) as i:
                act.wait_ge(pq_ready, i + 1)
                for s in range(SLOTS):
                    for j in range(GT):
                        t = s * GT + j
                        act.wait_ge(tile_done[1][j], i * SLOTS + (FREE + s))
                        a = nc.scalar.activation(sq_pq[:, j, 0:P], iota_p[:, :], ACT.Square, bias=pq_f[:, 0, t:t + 1])
                        a.then_inc(act_step, 1)
                        a = nc.scalar.activation(sq_pq[:, j, P:P + PQ], iota_q, ACT.Square, bias=pq_f[:, 1, t:t + 1])
                        a.then_inc(act_step, 1)
                        if t == TURN - 1:
                            act.wait_ge(act_step, (i + 1) * (2 * TURN))
                        else:
                            act.wait_ge(act_step, i * (2 * TURN) + 2 * (t + 1))
                        nc.scalar.activation(oh_pq[:, j, :], sq_pq[:, j, :], ACT.Relu, bias=one[:, :], scale=-1.0).then_inc(cnt_ready, 1)
                act.wait_ge(cnt_ready, (i + 1) * TURN)
                act.sem_inc(pq_used, 1)

        @block.vector
        def _(dve):
            count = [0]

            def link(ins):
                count[0] += 1
                ins.then_inc(dve_step, 1)
                dve.wait_ge(dve_step, count[0])

            nc.vector.memset(xs[:, WHOLE, :], 0.0).then_inc(tail_zero, 1)
            nc.vector.memset(w_bd[0][:, :, :], 0.0)
            link(nc.vector.memset(w_bd[1][:, :, :], 0.0))
            dve.sem_inc(bd_zero, 1)
            nc.vector.memset(zero[:, :], 0.0)
            for u in range(NB):
                nc.vector.memset(centers[:, u:u + 1], float(np.linspace(-1.0, 1.0, NB, dtype=np.float32)[u]))
            link(nc.vector.memset(one[:, :], 1.0))
            dve.sem_inc(consts_made, 1)
            dve.wait_ge(iota_made, 4)
            nc.vector.tensor_tensor(ident[:, :], iota_p[:, :], iota_row[:, :], ALU.is_equal).then_inc(ident_made, 1)
            dve.wait_ge(w_loads, 3 * 16)
            for l in (0, 1):
                last = nc.vector.tensor_copy(w_row[:, l, 0:KF].rearrange("i (o k) -> i o k", k=K),
                                             w_nat[:, l, :, :].rearrange("i k o -> i o k"))
            last.then_inc(w_rows, 1)
            dve.wait_ge(loads, 16 * N_LOADS)

            def node_view(t):
                return t[:, :, :].rearrange("p b (l f) -> p (b l) f", f=F)

            def over_features(i):
                return stat[:, i, :].unsqueeze(2).to_broadcast([P, PQ, F])

            for l in (0, 1):
                for s in range(SLOTS):
                    dve.sem_inc(rows_used[l][s], FREE)
                link(nc.vector.tensor_reduce(stat[:, 0, :], node_view(xs), AX.X, ALU.add))
                link(nc.vector.tensor_scalar(stat[:, 0, :], stat[:, 0, :], 1.0 / F, None, ALU.mult))
                link(nc.vector.tensor_tensor(node_view(hs), node_view(xs), over_features(0), ALU.subtract))
                link(nc.vector.tensor_tensor(sq[:, :, :], hs[:, :, :], hs[:, :, :], ALU.mult))
                link(nc.vector.tensor_reduce(stat[:, 1, :], node_view(sq), AX.X, ALU.add))
                nc.vector.tensor_scalar(stat[:, 1, :], stat[:, 1, :], 1.0 / F, EPS, ALU.mult, ALU.add).then_inc(var_ready, 1)
                dve.wait_ge(sd_ready, l + 1)
                link(nc.vector.reciprocal(stat[:, 0, :], stat[:, 2, :]))
                link(nc.vector.tensor_tensor(node_view(hs), node_view(hs), over_features(0), ALU.mult))
                link(nc.vector.tensor_scalar(hs[:, :, :], hs[:, :, :], 0.0, None, ALU.max))
                with dve.Fori(0, BLOCKS) as c:
                    dve.wait_ge(blk_turned[l], FREE + c)
                    nc.vector.tensor_copy(h_blk[:, :], hs[:, ds(c, 1), :].rearrange("p a c -> p (a c)")).then_inc(blk_ready[l], 1)

                base = count[0]
                per_turn = [0]

                def edge_turn(i, steps):
                    at = [0]

                    def chain(ins):
                        at[0] += 1
                        ins.then_inc(dve_step, 1)
                        dve.wait_ge(dve_step, i * steps + (base + at[0]))

                    to = ends[1 - l][:, ds(i * TURN, TURN)]
                    nc.vector.tensor_scalar(tgt_i[:, 0, :], to, 3, None, ALU.logical_shift_right)
                    if l == 1:
                        nc.vector.tensor_scalar(tgt_i[:, 2, :], to, 3, P - 1, ALU.logical_shift_right, ALU.bitwise_and)
                        nc.vector.tensor_scalar(tgt_i[:, 3, :], to, 10, 3, ALU.logical_shift_right, ALU.logical_shift_left)
                    chain(nc.vector.tensor_scalar(tgt_i[:, 1, :], to, LO - 1, None, ALU.bitwise_and))
                    nc.vector.tensor_copy(hi_f[:, :], tgt_i[:, 0, :])
                    chain(nc.vector.tensor_copy(lo_f[:, :], tgt_i[:, 1, :]))
                    chain(nc.vector.tensor_tensor(oh_lo[:, :, :], lo_f[:, :].unsqueeze(2).to_broadcast([P, TURN, LO]),
                                                  iota_lo[:, :].unsqueeze(1).to_broadcast([P, TURN, LO]), ALU.is_equal))
                    if l == 1:
                        dve.wait_ge(pq_used, FREE + i)
                        nc.vector.tensor_scalar(pq_f[:, 0, :], tgt_i[:, 2, :], -1.0, None, ALU.mult)
                        chain(nc.vector.tensor_tensor(pq_f[:, 1, :], tgt_i[:, 3, :], lo_f[:, :], ALU.add))
                        chain(nc.vector.tensor_scalar(pq_f[:, 1, :], pq_f[:, 1, :], -1.0, None, ALU.mult))
                        dve.sem_inc(pq_ready, 1)
                    if l == 0:
                        h3 = hats[:, :, :, :].rearrange("p t a u -> p (t a) u")
                        chain(nc.vector.tensor_tensor(h3, ea2[:, ds(i * (2 * TURN), 2 * TURN)].unsqueeze(2).to_broadcast([P, 2 * TURN, NB]),
                                                      centers[:, :].unsqueeze(1).to_broadcast([P, 2 * TURN, NB]), ALU.subtract))
                        chain(nc.vector.tensor_scalar(h3, h3, (NB - 1) / 2.0, None, ALU.mult))
                        chain(nc.vector.scalar_tensor_tensor(out=h3, in0=h3, scalar=-1.0, in1=h3, op0=ALU.mult, op1=ALU.min))
                        chain(nc.vector.tensor_scalar(h3, h3, 1.0, 0.0, ALU.add, ALU.max))
                        chain(nc.vector.tensor_tensor(coef0[:, :, :].rearrange("p t (u v) -> p t u v", v=NB),
                                                      hats[:, :, 0, :].unsqueeze(3).to_broadcast([P, TURN, NB, NB]),
                                                      hats[:, :, 1, :].unsqueeze(2).to_broadcast([P, TURN, NB, NB]), ALU.mult))
                    for s in range(SLOTS):
                        dve.wait_ge(rows_here[l][s], (i + 1) * (16 * GT))
                        if l == 1:
                            dve.wait_ge(coef_here[s], (i + 1) * 16)
                        c = coef0[:, s * GT:(s + 1) * GT, :] if l == 0 else coef1[:, s, :, :]
                        chain(nc.vector.tensor_tensor(prod[:, :, :, :], g[:, s, :, 0:KF].rearrange("p t (o k) -> p t o k", k=K),
                                                      c.unsqueeze(2).to_broadcast([P, GT, F, K]), ALU.mult))
                        m = msg[:, 0, :, :]
                        chain(nc.vector.tensor_reduce(m, prod[:, :, :, :], AX.X, ALU.add))
                        if l == 1:
                            chain(nc.vector.tensor_tensor(m, m, g[:, s, :, KF:KF + F], ALU.add))
                        dve.sem_inc(rows_used[l][s], 1)
                        chain(nc.vector.tensor_copy(part[:, 0, :, :], m))
                        chain(nc.vector.tensor_tensor(msg[:, 1, :, :], m, part[:, 0, :, :], ALU.subtract))
                        chain(nc.vector.tensor_copy(part[:, 1, :, :], msg[:, 1, :, :]))
                        chain(nc.vector.tensor_tensor(part[:, 2, :, :], msg[:, 1, :, :], part[:, 1, :, :], ALU.subtract))
                        for q in range(PARTS):
                            last = nc.vector.tensor_tensor(
                                lhs[:, s, q, :, :].rearrange("p t (l f) -> p t l f", f=F),
                                oh_lo[:, s * GT:(s + 1) * GT, :].unsqueeze(3).to_broadcast([P, GT, LO, F]),
                                part[:, q, :, :].unsqueeze(2).to_broadcast([P, GT, LO, F]), ALU.mult)
                        last.then_inc(lhs_ready[l], 1)
                        for j in range(GT):
                            dve.wait_ge(tile_done[l][j], i * SLOTS + (FREE + s))
                            nc.vector.tensor_scalar(oh_hi[:, j, :, :].rearrange("p b c -> p (b c)"), iota_hi[:, :],
                                                    hi_f[:, s * GT + j:s * GT + j + 1], None, ALU.is_equal).then_inc(hi_ready[l], 1)
                    return at[0]

                steps = (3 + 5 + SLOTS * 6) if l == 0 else (3 + 2 + SLOTS * 7)
                with dve.Fori(0, TURNS) as i:
                    assert edge_turn(i, steps) == steps
                count[0] = base + steps * TURNS
                dve.wait_ge(acc_done[l], 1)
                link(nc.vector.memset(acc_sb[:, BANKS * HC:], 0.0))
                link(nc.vector.tensor_copy(acc_sb[:, 0:BANKS * HC].rearrange("p (b c) -> p b c", b=BANKS), acc[:, :, 0:HC]))
                dve.sem_inc(acc_copied[l], 1)
                if l == 1:
                    link(nc.vector.tensor_scalar(stat[:, 0, :], cnt[:, 0:PQ], 1.0, None, ALU.max))
                    link(nc.vector.reciprocal(stat[:, 1, :], stat[:, 0, :]))
                for c in range(BLOCKS):
                    dve.wait_ge(sums_turned[l], c + 1)
                    src = ps_g[:, c % 2, 0:P]
                    if l == 0:
                        nc.vector.tensor_tensor(xs[:, c, :], xs[:, c, :], src, ALU.add).then_inc(sums_added[l], 1)
                    else:
                        nc.vector.tensor_copy(hs[:, c, :], src).then_inc(sums_added[l], 1)
                dve.wait_ge(sums_added[l], BLOCKS)
            link(nc.vector.tensor_tensor(node_view(hs), node_view(hs), over_features(1), ALU.mult))
            link(nc.vector.tensor_tensor(node_view(hs), node_view(hs), bias_rows[:, :].unsqueeze(1).to_broadcast([P, PQ, F]), ALU.add))
            nc.vector.tensor_tensor(hs[:, :, :], hs[:, :, :], xs[:, :, :], ALU.add).then_inc(x_final, 1)

        @block.tensor
        def _(pe):
            pe.wait_ge(ident_made, 1)
            pe.wait_ge(consts_made, 1)
            pe.wait_ge(bd_here, 2 * LO * 16)
            for l in (0, 1):
                pe.sem_inc(blk_turned[l], FREE)
                pe.sem_inc(g_made[l], FREE)
                for j in range(GT):
                    pe.sem_inc(tile_done[l][j], FREE)
                with pe.Fori(0, BLOCKS) as c:
                    pe.wait_ge(blk_ready[l], c + 1)
                    pe.wait_ge(hT_ready[l], FREE + c)
                    nc.tensor.transpose(ps_t[:, 0:P], h_blk[:, :], ident[:, :]).then_inc(blk_turned[l], 1)
                    pe.wait_ge(hT_ready[l], c + (FREE + 1))
                    for lo in range(LO):
                        pe.wait_ge(g_copied[l][lo % 2], c * (LO // 2) + (FREE + lo // 2))
                        nc.tensor.matmul(ps_g[:, lo % 2, 0:ROW[l]], hT[:, :], w_bd[l][:, lo, :],
                                         start=True, stop=True).then_inc(g_made[l], 1)
                for b in range(BANKS):
                    nc.tensor.matmul(acc[:, b, 0:HC], zero[:, 0:P], zero[:, :], start=True, stop=False)
                if l == 1:
                    nc.tensor.matmul(cnt[:, 0:PQ], zero[:, 0:P], zero[:, 0:PQ], start=True, stop=False)
                with pe.Fori(0, TURNS) as i:
                    for s in range(SLOTS):
                        pe.wait_ge(lhs_ready[l], i * SLOTS + s + 1)
                        for j in range(GT):
                            pe.wait_ge(hi_ready[l], i * TURN + s * GT + j + 1)
                            if l == 1:
                                pe.wait_ge(cnt_ready, i * TURN + s * GT + j + 1)
                                nc.tensor.matmul(cnt[:, 0:PQ], oh_pq[:, j, 0:P], oh_pq[:, j, P:P + PQ], start=False, stop=False)
                            for q in range(PARTS):
                                for b in range(BANKS):
                                    last = nc.tensor.matmul(acc[:, b, 0:HC], lhs[:, s, q, j, :], oh_hi[:, j, b, :],
                                                            start=False, stop=False)
                            last.then_inc(tile_done[l][j], 1)
                if l == 1:
                    nc.tensor.matmul(cnt[:, 0:PQ], zero[:, 0:P], zero[:, 0:PQ], start=False, stop=True)
                for b in range(BANKS):
                    last = nc.tensor.matmul(acc[:, b, 0:HC], zero[:, 0:P], zero[:, :], start=False, stop=True)
                last.then_inc(acc_done[l], 1)
                pe.wait_ge(acc_copied[l], 1)
                for c in range(BLOCKS):
                    if c >= 2:
                        pe.wait_ge(sums_added[l], c - 1)
                    nc.tensor.transpose(ps_g[:, c % 2, 0:P], acc_sb[:, c * P:(c + 1) * P], ident[:, :]).then_inc(sums_turned[l], 1)


_INS = ["x", "src", "dst", "edge_attr_16", "edge_attr_2", "L0_gnn_weight", "L1_gnn_W_e", "L1_gnn_b_e", "L1_gnn_bias"]


def kernel(**inputs):
    import concourse.bacc as bacc
    from concourse.bass_utils import run_bass_kernel_spmd

    nc = bacc.Bacc("TRN2", target_bir_lowering=False, num_devices=1)
    arrays, args = {}, []
    for name in _INS:
        a = np.ascontiguousarray(inputs[name])
        arrays[f"in_{name}"] = a
        args.append(nc.dram_tensor(f"in_{name}", a.shape, mybir.dt.from_np(a.dtype), kind="ExternalInput").ap())
    out = nc.dram_tensor("out", (N_NODES, F), mybir.dt.float32, kind="ExternalOutput").ap()
    build(nc, *args, out)
    r = run_bass_kernel_spmd(nc, [arrays], core_ids=[0])
    return r.results[0]["out"]
```

```python
from contextlib import ExitStack

import concourse.bass as bass
import numpy as np
from concourse import mybir

P = 128
N_NODES, N_EDGES, F = 12500, 400000, 16
LO = P // F
BLOCKS = -(-N_NODES // (P * LO))
PADDED = BLOCKS * P * LO
WHOLE = N_NODES // (P * LO)
TAIL_P = (N_NODES - WHOLE * P * LO) // LO
TAIL_LO = N_NODES - WHOLE * P * LO - TAIL_P * LO
HI = -(-N_NODES // LO)
BANKS = 4
HC = -(-HI // BANKS)
TILES = N_EDGES // P
GT = 5
SLOTS = 5
TURN = GT * SLOTS
TURNS = TILES // TURN
RING = 2 * GT
GB = 4
K = 16
NB = 4
PARTS = 2
KF = K * F
ROW = [KF, KF + F]
EPS = 1e-5
SCALE = [2.0 ** 10, 2.0 ** 6]
M_LEAST, M_MOST = 2.0 ** -100, 2.0 ** 110
EXPONENT_BITS = 0x7F800000
PQ = BLOCKS * LO
FREE = 1


def build(nc, x_in, src_in, dst_in, ea16_in, ea2_in, w0_in, we_in, be_in, bias_in, out):
    fp32, bf16, fp16, i32 = mybir.dt.float32, mybir.dt.bfloat16, mybir.dt.float16, mybir.dt.int32
    ALU, ACT, AX = mybir.AluOpType, mybir.ActivationFunctionType, mybir.AxisListType
    MAX_ALL = bass.bass_isa.ReduceOp.max
    ds = bass.ds

    ctx = ExitStack()
    with ctx:
        def sb(name, shape, dt):
            return ctx.enter_context(nc.sbuf_tensor(name, shape, dt))

        def pb(name, shape, dt):
            return ctx.enter_context(nc.psum_tensor(name, shape, dt))

        def sem(name):
            return ctx.enter_context(nc.semaphore(name))

        table = [nc.dram_tensor(f"table{l}", (PADDED, ROW[l]), fp32, kind="Internal").ap() for l in (0, 1)]

        xs = sb("xs", [P, BLOCKS, P], fp32)
        hs = sb("hs", [P, BLOCKS, P], fp32)
        sq = sb("sq", [P, BLOCKS, P], fp32)
        stat = sb("stat", [P, 3, PQ], fp32)
        ends = [sb("dst_ids", [P, TILES], i32), sb("src_ids", [P, TILES], i32)]
        hi_all = sb("hi_all", [P, TILES], fp16)
        lo_all = sb("lo_all", [P, TILES], fp16)
        place_all = sb("place_all", [P, 2, TILES], fp16)
        ident = sb("ident", [P, P], fp32)
        iota_hi = sb("iota_hi", [P, BANKS * HC], fp16)
        iota_lo = sb("iota_lo", [P, LO], fp16)
        iota_p = sb("iota_p", [P, P], fp32)
        iota_row = sb("iota_row", [P, P], fp32)
        minus_center = sb("minus_center", [P, NB], fp32)
        zero = sb("zero", [P, HC], fp16)
        one = sb("one", [P, 1], fp32)
        bias_rows = sb("bias_rows", [P, F], fp32)
        w_nat = sb("w_nat", [F, 2, K, F], fp32)
        w_row = sb("w_row", [F, 2, ROW[1]], fp32)
        w_bd = sb("w_bd", [P, LO, ROW[1]], fp32)
        largest = sb("largest", [P, 4], fp32)
        largest_all = sb("largest_all", [P, 4], fp32)
        ea_max = sb("ea_max", [P, TURNS], fp32)
        pow2 = sb("pow2", [P, 2], fp32)
        scale = sb("scale", [P, 2], fp32)
        h_blk = sb("h_blk", [P, 2, P], fp32)
        hT = sb("hT", [P, 2, P], fp32)
        ids = sb("ids", [P, SLOTS, GT], i32)
        g = sb("g", [P, SLOTS, GT, ROW[1]], fp32)
        g_flat = g[:, :, :, :].rearrange("p s t r -> p (s t r)")
        coef1 = sb("coef1", [P, SLOTS, GT, K], fp32)
        ea2 = sb("ea2", [P, TURN * 2], fp32)
        distance = sb("distance", [P, TURN, 2, NB], fp32)
        hats = sb("hats", [P, TURN, 2, NB], fp32)
        coef0 = sb("coef0", [P, 2, TURN, K], fp32)
        prod = sb("prod", [P, GT, F, K], fp32)
        msg = sb("msg", [P, 2, GT, F], fp32)
        part = sb("part", [P, PARTS, GT, F], fp16)
        hi_f = sb("hi_f", [P, SLOTS, GT], fp32)
        place_f = sb("place_f", [P, SLOTS, 2, GT], fp32)
        oh_lo = sb("oh_lo", [P, 2, TURN, LO], fp16)
        wide_lo = sb("wide_lo", [P, SLOTS, GT, P], fp16)
        lhs = sb("lhs", [P, SLOTS, PARTS, GT, P], fp16)
        oh_hi = sb("oh_hi", [P, RING, BANKS, HC], fp16)
        sq_place = sb("sq_place", [P, RING, P + PQ], bf16)
        oh_place = sb("oh_place", [P, RING, P + PQ], bf16)
        acc_sb = sq[:, :, :].rearrange("p b c -> p (b c)")
        id_bits = lhs[:, :, :, :, :].rearrange("p s q t c -> p (s q t c)").bitcast(i32)[:, 0:TILES]

        acc = pb("acc", [P, BANKS, 512], fp32)
        cnt = pb("cnt", [P, 512], fp32)
        ps_s = pb("ps_s", [P, 2, 512], fp32)

        x_loads, id_loads, bias_load = sem("x_loads"), sem("id_loads"), sem("bias_load")
        w_loads, w_rows, bd_zero = sem("w_loads"), sem("w_rows"), sem("bd_zero")
        iota_made, ident_made, consts_made, tail_zero = (
            sem("iota_made"), sem("ident_made"), sem("consts_made"), sem("tail_zero"))
        dve_step = sem("dve_step")
        act_step, ids_settled, blk_settled = sem("act_step"), sem("ids_settled"), sem("blk_settled")
        var_ready, sd_ready = sem("var_ready"), sem("sd_ready")
        largest_ready, largest_shared, scale_ready = sem("largest_ready"), sem("largest_shared"), sem("scale_ready")

        def by_layer(name):
            return [sem(f"{name}{l}") for l in (0, 1)]

        def by_slot(name, n):
            return [[sem(f"{name}{l}_{s}") for s in range(n)] for l in (0, 1)]

        bd_here, blk_ready, blk_turned, hT_ready, g_made = map(
            by_layer, ("bd_here", "blk_ready", "blk_turned", "hT_ready", "g_made"))
        g_copied, rows_stored = by_slot("g_copied", GB), by_slot("rows_stored", 2)
        targets_ready, ids_ready, lo_ready, hi_staged, wide_ready, lhs_ready, hi_ready = map(
            by_layer, ("targets_ready", "ids_ready", "lo_ready", "hi_staged", "wide_ready", "lhs_ready", "hi_ready"))
        rows_here, rows_used = by_slot("rows_here", SLOTS), by_slot("rows_used", SLOTS)
        tile_done = by_slot("tile_done", RING)
        coef_here = [sem(f"coef_here_{s}") for s in range(SLOTS)]
        ea_here, ea_used = sem("ea_here"), sem("ea_used")
        ea2_here, distance_made, hats_ready, coef0_made = sem("ea2_here"), sem("distance_made"), sem("hats_ready"), sem("coef0_made")
        place_staged, places_squared, cnt_ready = sem("place_staged"), sem("places_squared"), sem("cnt_ready")
        acc_done, acc_copied, sums_turned, sums_added = map(
            by_layer, ("acc_done", "acc_copied", "sums_turned", "sums_added"))
        x_final, stored = sem("x_final"), sem("stored")

        def paired(eng, n, body):
            with eng.Fori(0, n // 2) as k:
                body(k, 0)
                body(k, 1)
            body(n // 2, 0)

        def ring_slot(par, s, j):
            tile = par * TURN + s * GT + j
            return tile % RING, tile // RING

        ROUND = 2 * TURN // RING

        block = ctx.enter_context(nc.Block())
        top = WHOLE * P * LO

        @block.sync
        def _(sp):
            sp.wait_ge(tail_zero, 1)
            sp.dma_start(xs[:, 0:WHOLE, :], x_in[0:top, :].rearrange("(c p l) f -> p c (l f)", p=P, l=LO)).then_inc(x_loads, 16)
            sp.dma_start(xs[0:TAIL_P, WHOLE, :], x_in[top:top + TAIL_P * LO, :].rearrange("(p l) f -> p (l f)", l=LO)).then_inc(x_loads, 16)
            sp.dma_start(xs[TAIL_P:TAIL_P + 1, WHOLE, 0:TAIL_LO * F],
                         x_in[top + TAIL_P * LO:N_NODES, :].rearrange("(p l) f -> p (l f)", l=TAIL_LO)).then_inc(x_loads, 16)
            sp.dma_start(w_nat[:, 0, :, :], w0_in.rearrange("u v i o -> i (u v) o")).then_inc(w_loads, 16)
            sp.dma_start(w_nat[:, 1, :, :], we_in.rearrange("d (i o) -> i d o", o=F)).then_inc(w_loads, 16)
            sp.dma_start(w_row[:, 1, KF:KF + F], be_in.rearrange("(i o) -> i o", o=F)).then_inc(w_loads, 16)
            sp.dma_start(ends[1][:, :], src_in.rearrange("(p t) -> p t", p=P)).then_inc(id_loads, 16)
            sp.dma_start(ends[0][:, :], dst_in.rearrange("(p t) -> p t", p=P)).then_inc(id_loads, 16)
            sp.dma_start(bias_rows[:, :], bias_in.rearrange("(a o) -> a o", a=1).to_broadcast([P, F])).then_inc(bias_load, 16)
            ea = ea16_in.rearrange("(p t) d -> p (t d)", p=P)
            ea2_all = ea2_in.rearrange("(p t) c -> p (t c)", p=P)
            sp.wait_ge(w_rows, 1)
            sp.wait_ge(bd_zero, 1)
            for l in (0, 1):
                if l == 1:
                    sp.wait_ge(g_made[0], (BLOCKS + 2) * LO)
                for lo in range(LO):
                    sp.dma_start(w_bd[F * lo:F * lo + F, lo, 0:ROW[l]], w_row[:, l, 0:ROW[l]]).then_inc(bd_here[l], 16)
                if l == 1:
                    with sp.Fori(0, TURNS) as i:
                        sp.wait_ge(distance_made, FREE + i)
                        sp.dma_start(ea2[:, :], ea2_all[:, ds(i * (TURN * 2), TURN * 2)]).then_inc(ea2_here, 16)
                        sp.wait_ge(ea_used, FREE + i)
                        sp.dma_start(coef1[:, :, :, :].rearrange("p s t d -> p (s t d)"),
                                     ea[:, ds(i * (TURN * K), TURN * K)]).then_inc(ea_here, 16)
                    sp.wait_ge(ea_used, FREE + TURNS)
                rows = table[l].rearrange("(c p l) r -> c p (l r)", p=P, l=LO)

                def store_block(k, par):
                    c = k * 2 + par
                    for b in range(GB):
                        sp.wait_ge(g_copied[l][b], (c + 1) * (LO // GB) + FREE)
                    sp.dma_start(rows[ds(c, 1), :, :].rearrange("a p r -> (a p) r"),
                                 g_flat[:, par * LO * ROW[1]:par * LO * ROW[1] + LO * ROW[l]]).then_inc(rows_stored[l][par], 16)

                paired(sp, BLOCKS, store_block)
            with sp.Fori(0, TURNS) as i:
                for s in range(SLOTS):
                    sp.wait_ge(rows_used[1][s], FREE + i)
                    sp.dma_start(coef1[:, s, :, :].rearrange("p t d -> p (t d)"),
                                 ea[:, ds(i * (TURN * K) + s * GT * K, GT * K)]).then_inc(coef_here[s], 16)
            sp.wait_ge(x_final, 1)
            sp.dma_start(out[0:top, :].rearrange("(c p l) f -> p c (l f)", p=P, l=LO), hs[:, 0:WHOLE, :]).then_inc(stored, 16)
            sp.dma_start(out[top:top + TAIL_P * LO, :].rearrange("(p l) f -> p (l f)", l=LO), hs[0:TAIL_P, WHOLE, :]).then_inc(stored, 16)
            sp.dma_start(out[top + TAIL_P * LO:N_NODES, :].rearrange("(p l) f -> p (l f)", l=TAIL_LO),
                         hs[TAIL_P:TAIL_P + 1, WHOLE, 0:TAIL_LO * F]).then_inc(stored, 16)
            sp.wait_ge(stored, 3 * 16)

        @block.gpsimd
        def _(pool):
            def iota(t, pattern, channel_multiplier):
                nc.gpsimd.iota(t, pattern, base=0, channel_multiplier=channel_multiplier,
                               allow_small_or_imprecise_dtypes=True).then_inc(iota_made, 1)

            iota(iota_p[:, :], [[1, P]], 0)
            iota(iota_row[:, :], [[0, P]], 1)
            iota(iota_lo[:, :], [[1, LO]], 0)
            iota(iota_hi[:, :], [[1, BANKS * HC]], 0)
            for l in (0, 1):
                pool.wait_ge(largest_ready, l + 1)
                nc.gpsimd.partition_all_reduce(largest_all[:, 3 * l:3 + l], largest[:, 3 * l:3 + l], P, MAX_ALL).then_inc(largest_shared, 1)
                pool.wait_ge(id_loads, 2 * 16)
                for par in (0, 1):
                    pool.wait_ge(rows_stored[l][par], 16 * (FREE + (BLOCKS + 1 - par) // 2))
                with pool.Fori(0, TURNS) as i:
                    for s in range(SLOTS):
                        pool.wait_ge(rows_used[l][s], FREE + i)
                        nc.gpsimd.tensor_copy(ids[:, s, :], ends[l][:, ds(i * TURN + s * GT, GT)]).then_inc(ids_ready[l], 1)
                        pool.wait_ge(ids_ready[l], i * SLOTS + s + 1)
                        pool.sem_inc(ids_settled, 1)
                        for j in range(GT):
                            nc.gpsimd.indirect_dma_start(
                                out=g[:, s, j, 0:ROW[l]], out_offset=None, in_=table[l],
                                in_offset=bass.IndirectOffsetOnAxis(ap=ids[:, s, j:j + 1], axis=0),
                            ).then_inc(rows_here[l][s], 16)

        @block.scalar
        def _(act):
            def hat_functions(i):
                act.wait_ge(coef0_made, FREE + i)
                act.wait_ge(ea2_here, (i + 1) * 16)
                for u in range(NB):
                    a = nc.scalar.activation(distance[:, :, :, u].rearrange("p t a -> p (t a)"), ea2[:, :], ACT.Abs,
                                             bias=minus_center[:, u:u + 1])
                a.then_inc(distance_made, 1)
                act.wait_ge(distance_made, FREE + i + 1)
                nc.scalar.activation(hats[:, :, :, :], distance[:, :, :, :], ACT.Relu, bias=one[:, :],
                                     scale=-(NB - 1) / 2.0).then_inc(hats_ready, 1)

            act.wait_ge(consts_made, 1)
            act.sem_inc(distance_made, FREE)
            for l in (0, 1):
                for par in (0, 1):
                    act.sem_inc(rows_stored[l][par], 16 * FREE)
                for b in range(GB):
                    act.sem_inc(g_copied[l][b], FREE)
                act.sem_inc(hT_ready[l], 2)
                act.wait_ge(var_ready, l + 1)
                nc.scalar.activation(stat[:, 2, :], stat[:, 1, :], ACT.Sqrt).then_inc(sd_ready, 1)
                act.wait_ge(scale_ready, l + 1)

                def copy_rows(k, par):
                    c = k * 2 + par
                    act.wait_ge(blk_turned[l], c + 3)
                    act.wait_ge(g_made[l], (c + 1) * LO)
                    nc.scalar.copy(hT[:, par, :], ps_s[:, par, 0:P]).then_inc(hT_ready[l], 1)
                    act.wait_ge(rows_stored[l][par], (k + FREE) * 16)
                    for lo in range(0, LO, 2):
                        act.wait_ge(g_made[l], c * LO + (2 * LO + lo + 1))
                        at = par * LO * ROW[1] + lo * ROW[l]
                        nc.scalar.activation(g_flat[:, at:at + ROW[l]], acc[:, lo % GB, 0:ROW[l]], ACT.Copy,
                                             scale=scale[:, l:l + 1]).then_inc(g_copied[l][lo % GB], 1)

                paired(act, BLOCKS, copy_rows)
                act.wait_ge(targets_ready[l], 1)
                if l == 0:
                    hat_functions(0)

                def edge_turn(k, par):
                    i = k * 2 + par
                    act.wait_ge(lo_ready[l], i + 1)
                    for s in range(SLOTS):
                        act.wait_ge(hi_ready[l], i * TURN + (s + 1) * GT)
                        act.sem_inc(act_step, 1)
                        tiles = ds(i * TURN + s * GT, GT)
                        nc.scalar.copy(hi_f[:, s, :], hi_all[:, tiles]).then_inc(hi_staged[l], 1)
                        nc.scalar.copy(wide_lo[:, s, :, :].rearrange("p t (l f) -> p (t l) f", f=F),
                                       oh_lo[:, par, s * GT:(s + 1) * GT, :].rearrange("p t l -> p (t l)").unsqueeze(2)
                                       .to_broadcast([P, GT * LO, F])).then_inc(wide_ready[l], 1)
                        if l == 0 and s == 1 and not (isinstance(k, int) and i == TURNS - 1):
                            hat_functions(i + 1)
                        if l == 1:
                            nc.scalar.mul(place_f[:, s, :, :], place_all[:, :, tiles], -1.0).then_inc(place_staged, 1)
                            act.wait_ge(place_staged, i * SLOTS + s + 1)
                            for j in range(GT):
                                r, before = ring_slot(par, s, j)
                                act.wait_ge(tile_done[1][r], k * ROUND + (FREE + before))
                                nc.scalar.activation(sq_place[:, r, 0:P], iota_p[:, :], ACT.Square, bias=place_f[:, s, 0, j:j + 1])
                                nc.scalar.activation(sq_place[:, r, P:P + PQ], iota_p[:, 0:PQ], ACT.Square,
                                                     bias=place_f[:, s, 1, j:j + 1]).then_inc(places_squared, 1)
                                act.wait_ge(places_squared, i * TURN + s * GT + j + 1)
                                nc.scalar.activation(oh_place[:, r, :], sq_place[:, r, :], ACT.Relu, bias=one[:, :], scale=-1.0).then_inc(cnt_ready, 1)

                paired(act, TURNS, edge_turn)

        @block.vector
        def _(dve):
            count = [0]

            def link(ins):
                count[0] += 1
                ins.then_inc(dve_step, 1)
                dve.wait_ge(dve_step, count[0])

            nc.vector.memset(xs[:, WHOLE, :], 0.0).then_inc(tail_zero, 1)
            nc.vector.memset(w_bd[:, :, :], 0.0).then_inc(bd_zero, 1)
            nc.vector.memset(zero[:, :], 0.0)
            for u in range(NB):
                nc.vector.memset(minus_center[:, u:u + 1], -float(np.linspace(-1.0, 1.0, NB, dtype=np.float32)[u]))
            link(nc.vector.memset(one[:, :], 1.0))
            dve.sem_inc(consts_made, 1)
            dve.wait_ge(iota_made, 4)
            nc.vector.tensor_tensor(ident[:, :], iota_p[:, :], iota_row[:, :], ALU.is_equal).then_inc(ident_made, 1)
            dve.wait_ge(w_loads, 3 * 16)
            for l in (0, 1):
                last = nc.vector.tensor_copy(w_row[:, l, 0:KF].rearrange("i (o k) -> i o k", k=K),
                                             w_nat[:, l, :, :].rearrange("i k o -> i o k"))
            last.then_inc(w_rows, 1)
            link(nc.vector.memset(largest[:, :], 0.0))
            nc.vector.tensor_reduce(largest[0:F, 0:2], w_nat[:, :, :, :].rearrange("i l k o -> i l (k o)"), AX.X, ALU.max,
                                    apply_absolute_value=True)
            link(nc.vector.tensor_reduce(largest[0:F, 2:3], w_row[:, 1, KF:KF + F], AX.X, ALU.max, apply_absolute_value=True))
            dve.sem_inc(largest_ready, 1)
            dve.wait_ge(x_loads, 3 * 16)

            def node_view(t):
                return t[:, :, :].rearrange("p b (l f) -> p (b l) f", f=F)

            def over_features(i):
                return stat[:, i, :].unsqueeze(2).to_broadcast([P, PQ, F])

            dve.sem_inc(ea_used, FREE)
            dve.sem_inc(coef0_made, FREE)
            for l in (0, 1):
                for s in range(SLOTS):
                    dve.sem_inc(rows_used[l][s], FREE)
                dve.sem_inc(hi_ready[l], TURN)
                link(nc.vector.tensor_reduce(stat[:, 0, :], node_view(xs), AX.X, ALU.add))
                link(nc.vector.tensor_scalar(stat[:, 0, :], stat[:, 0, :], 1.0 / F, None, ALU.mult))
                link(nc.vector.tensor_tensor(node_view(hs), node_view(xs), over_features(0), ALU.subtract))
                link(nc.vector.tensor_tensor(sq[:, :, :], hs[:, :, :], hs[:, :, :], ALU.mult))
                link(nc.vector.tensor_reduce(stat[:, 1, :], node_view(sq), AX.X, ALU.add))
                nc.vector.tensor_scalar(stat[:, 1, :], stat[:, 1, :], 1.0 / F, EPS, ALU.mult, ALU.add).then_inc(var_ready, 1)
                dve.wait_ge(sd_ready, l + 1)
                link(nc.vector.reciprocal(stat[:, 0, :], stat[:, 2, :]))
                link(nc.vector.tensor_tensor(node_view(hs), node_view(hs), over_features(0), ALU.mult))
                link(nc.vector.tensor_scalar(hs[:, :, :], hs[:, :, :], 0.0, None, ALU.max))
                dve.wait_ge(largest_shared, l + 1)
                big = largest_all[:, l:l + 1]
                if l == 1:
                    link(nc.vector.tensor_tensor(big, big, largest_all[:, 2:3], ALU.max))
                    link(nc.vector.tensor_scalar(largest_all[:, 3:4], largest_all[:, 3:4], 1.0, None, ALU.max))
                    link(nc.vector.tensor_tensor(big, big, largest_all[:, 3:4], ALU.mult))
                p2 = pow2[:, l:l + 1]
                link(nc.vector.tensor_scalar(p2, big, M_LEAST, M_MOST, ALU.max, ALU.min))
                link(nc.vector.tensor_scalar(p2.bitcast(i32), p2.bitcast(i32), EXPONENT_BITS, None, ALU.bitwise_and))
                link(nc.vector.tensor_scalar(p2, p2, 1.0 / SCALE[l], None, ALU.mult))
                link(nc.vector.reciprocal(scale[:, l:l + 1], p2))
                dve.sem_inc(scale_ready, 1)

                def hand_block(c, par):
                    dve.wait_ge(blk_turned[l], c + 1)
                    dve.sem_inc(blk_settled, 1)
                    nc.vector.tensor_copy(h_blk[:, par, :], hs[:, ds(c, 1), :].rearrange("p a c -> p (a c)")).then_inc(blk_ready[l], 1)

                def copy_rows(k, par):
                    c = k * 2 + par
                    if not (isinstance(k, int) and c == BLOCKS - 1):
                        hand_block(c + 1, 1 - par)
                    dve.wait_ge(rows_stored[l][par], (k + FREE) * 16)
                    for lo in range(1, LO, 2):
                        dve.wait_ge(g_made[l], c * LO + (2 * LO + lo + 1))
                        at = par * LO * ROW[1] + lo * ROW[l]
                        nc.vector.tensor_scalar(g_flat[:, at:at + ROW[l]], acc[:, lo % GB, 0:ROW[l]], scale[:, l:l + 1], None,
                                                ALU.mult).then_inc(g_copied[l][lo % GB], 1)

                hand_block(0, 0)
                paired(dve, BLOCKS, copy_rows)

                if l == 0:
                    dve.wait_ge(id_loads, 2 * 16)
                to, bits = ends[1 - l][:, :], id_bits
                link(nc.vector.tensor_scalar(bits, to, 3, None, ALU.logical_shift_right))
                link(nc.vector.tensor_copy(hi_all[:, :], bits))
                link(nc.vector.tensor_scalar(bits, to, LO - 1, None, ALU.bitwise_and))
                link(nc.vector.tensor_copy(lo_all[:, :], bits))
                if l == 1:
                    link(nc.vector.tensor_scalar(bits, to, 3, P - 1, ALU.logical_shift_right, ALU.bitwise_and))
                    link(nc.vector.tensor_copy(place_all[:, 0, :], bits))
                    link(nc.vector.tensor_scalar(bits, to, 10, 3, ALU.logical_shift_right, ALU.logical_shift_left))
                    link(nc.vector.tensor_tensor(place_all[:, 1, :], bits, lo_all[:, :], ALU.add))
                dve.sem_inc(targets_ready[l], 1)

                def prepare(i, par):
                    nc.vector.tensor_tensor(oh_lo[:, par, :, :], lo_all[:, ds(i * TURN, TURN)].unsqueeze(2).to_broadcast([P, TURN, LO]),
                                            iota_lo[:, :].unsqueeze(1).to_broadcast([P, TURN, LO]), ALU.is_equal).then_inc(lo_ready[l], 1)
                    if l == 0:
                        dve.wait_ge(ea_here, (i + 1) * 16)
                        nc.vector.tensor_reduce(ea_max[:, ds(i, 1)], coef1[:, :, :, :].rearrange("p s t d -> p (s t d)"),
                                                AX.X, ALU.max, apply_absolute_value=True).then_inc(ea_used, 1)
                        dve.wait_ge(hats_ready, i + 1)
                        nc.vector.tensor_tensor(coef0[:, par, :, :].rearrange("p t (u v) -> p t u v", v=NB),
                                                hats[:, :, 0, :].unsqueeze(3).to_broadcast([P, TURN, NB, NB]),
                                                hats[:, :, 1, :].unsqueeze(2).to_broadcast([P, TURN, NB, NB]), ALU.mult).then_inc(coef0_made, 1)

                STEPS = SLOTS * (4 + l)
                base = count[0]

                def edge_turn(k, par):
                    i = k * 2 + par
                    is_last = isinstance(k, int) and i == TURNS - 1
                    at = [0]

                    def step(ins):
                        at[0] += 1
                        ins.then_inc(dve_step, 1)
                        return at[0]

                    def after(n):
                        dve.wait_ge(dve_step, i * STEPS + (base + n))

                    for s in range(SLOTS):
                        def hi_onehot(j):
                            r, before = ring_slot(par, s, j)
                            dve.wait_ge(tile_done[l][r], k * ROUND + (FREE + before))
                            nc.vector.tensor_scalar(oh_hi[:, r, :, :].rearrange("p b c -> p (b c)"), iota_hi[:, :],
                                                    hi_f[:, s, j:j + 1], None, ALU.is_equal).then_inc(hi_ready[l], 1)

                        def left_operand(q):
                            return nc.vector.tensor_tensor(
                                lhs[:, s, q, :, :].rearrange("p t (l f) -> p t l f", f=F),
                                wide_lo[:, s, :, :].rearrange("p t (l f) -> p t l f", f=F),
                                part[:, q, :, :].unsqueeze(2).to_broadcast([P, GT, LO, F]), ALU.mult)

                        dve.wait_ge(rows_here[l][s], (i + 1) * (16 * GT))
                        if l == 0:
                            if s == 0:
                                dve.wait_ge(coef0_made, FREE + i + 1)
                            c = coef0[:, par, s * GT:(s + 1) * GT, :]
                        else:
                            dve.wait_ge(coef_here[s], (i + 1) * 16)
                            c = coef1[:, s, :, :]
                        m = msg[:, 0, :, :]
                        multiplied = step(nc.vector.tensor_tensor(prod[:, :, :, :], g[:, s, :, 0:KF].rearrange("p t (o k) -> p t o k", k=K),
                                                                  c.unsqueeze(2).to_broadcast([P, GT, F, K]), ALU.mult))
                        dve.wait_ge(hi_staged[l], i * SLOTS + (s + 1))
                        hi_onehot(0)
                        after(multiplied)
                        if l == 0:
                            dve.sem_inc(rows_used[l][s], 1)
                        summed = step(nc.vector.tensor_reduce(m, prod[:, :, :, :], AX.X, ALU.add))
                        hi_onehot(1)
                        after(summed)
                        if l == 1:
                            summed = step(nc.vector.tensor_tensor(m, m, g[:, s, :, KF:KF + F], ALU.add))
                            hi_onehot(2)
                            after(summed)
                            dve.sem_inc(rows_used[l][s], 1)
                        rounded = step(nc.vector.tensor_copy(part[:, 0, :, :], m))
                        hi_onehot(2 + l)
                        after(rounded)
                        rest = step(nc.vector.tensor_tensor(part[:, 1, :, :], m, part[:, 0, :, :], ALU.subtract))
                        dve.wait_ge(wide_ready[l], i * SLOTS + (s + 1))
                        left_operand(0)
                        after(rest)
                        left_operand(1).then_inc(lhs_ready[l], 1)
                        for j in range(3 + l, GT):
                            hi_onehot(j)
                        if s == SLOTS - 2 and not is_last:
                            prepare(i + 1, 1 - par)
                    assert at[0] == STEPS

                prepare(0, 0)
                paired(dve, TURNS, edge_turn)
                count[0] = base + STEPS * TURNS
                if l == 0:
                    link(nc.vector.tensor_reduce(largest[:, 3:4], ea_max[:, :], AX.X, ALU.max))
                    dve.sem_inc(largest_ready, 1)
                dve.wait_ge(acc_done[l], 1)
                link(nc.vector.memset(acc_sb[:, BANKS * HC:], 0.0))
                link(nc.vector.tensor_copy(acc_sb[:, 0:BANKS * HC].rearrange("p (b c) -> p b c", b=BANKS), acc[:, :, 0:HC]))
                dve.sem_inc(acc_copied[l], 1)
                if l == 1:
                    link(nc.vector.tensor_scalar(stat[:, 0, :], cnt[:, 0:PQ], 1.0, None, ALU.max))
                    link(nc.vector.reciprocal(stat[:, 1, :], stat[:, 0, :]))
                for c in range(BLOCKS):
                    dve.wait_ge(sums_turned[l], c + 1)
                    src = ps_s[:, c % 2, 0:P]
                    if l == 0:
                        nc.vector.scalar_tensor_tensor(out=xs[:, c, :], in0=src, scalar=pow2[:, 0:1], in1=xs[:, c, :],
                                                       op0=ALU.mult, op1=ALU.add).then_inc(sums_added[l], 1)
                    else:
                        nc.vector.tensor_scalar(hs[:, c, :], src, pow2[:, 1:2], None, ALU.mult).then_inc(sums_added[l], 1)
                dve.wait_ge(sums_added[l], BLOCKS)
            dve.wait_ge(bias_load, 16)
            link(nc.vector.tensor_tensor(node_view(hs), node_view(hs), over_features(1), ALU.mult))
            link(nc.vector.tensor_tensor(node_view(hs), node_view(hs), bias_rows[:, :].unsqueeze(1).to_broadcast([P, PQ, F]), ALU.add))
            nc.vector.tensor_tensor(hs[:, :, :], hs[:, :, :], xs[:, :, :], ALU.add).then_inc(x_final, 1)

        @block.tensor
        def _(pe):
            pe.wait_ge(ident_made, 1)
            pe.wait_ge(consts_made, 1)
            for l in (0, 1):
                pe.sem_inc(blk_turned[l], 2)
                pe.sem_inc(g_made[l], 2 * LO)
                for r in range(RING):
                    pe.sem_inc(tile_done[l][r], FREE)
                pe.wait_ge(bd_here[l], LO * 16)

                def turn_block(c, par):
                    pe.wait_ge(blk_ready[l], c + 1)
                    pe.wait_ge(hT_ready[l], c + 1)
                    nc.tensor.transpose(ps_s[:, par, 0:P], h_blk[:, par, :], ident[:, :]).then_inc(blk_turned[l], 1)

                def make_rows(k, par):
                    c = k * 2 + par
                    if not (isinstance(k, int) and c == BLOCKS - 1):
                        turn_block(c + 1, 1 - par)
                    pe.wait_ge(hT_ready[l], c + 3)
                    for lo in range(LO):
                        pe.wait_ge(g_copied[l][lo % GB], c * (LO // GB) + (FREE + lo // GB))
                        nc.tensor.matmul(acc[:, lo % GB, 0:ROW[l]], hT[:, par, :], w_bd[:, lo, 0:ROW[l]],
                                         start=True, stop=True).then_inc(g_made[l], 1)

                turn_block(0, 0)
                paired(pe, BLOCKS, make_rows)
                for b in range(GB):
                    pe.wait_ge(g_copied[l][b], BLOCKS * (LO // GB) + FREE)
                for b in range(BANKS):
                    nc.tensor.matmul(acc[:, b, 0:HC], zero[:, 0:P], zero[:, :], start=True, stop=False)
                if l == 1:
                    nc.tensor.matmul(cnt[:, 0:PQ], zero[:, 0:P], zero[:, 0:PQ], start=True, stop=False)

                def edge_turn(k, par):
                    i = k * 2 + par
                    for s in range(SLOTS):
                        pe.wait_ge(lhs_ready[l], i * SLOTS + s + 1)
                        for j in range(GT):
                            r, _ = ring_slot(par, s, j)
                            pe.wait_ge(hi_ready[l], i * TURN + (TURN + s * GT + j + 1))
                            if l == 1:
                                pe.wait_ge(cnt_ready, i * TURN + s * GT + j + 1)
                                nc.tensor.matmul(cnt[:, 0:PQ], oh_place[:, r, 0:P], oh_place[:, r, P:P + PQ], start=False, stop=False)
                            for q in range(PARTS):
                                for b in range(BANKS):
                                    last = nc.tensor.matmul(acc[:, b, 0:HC], lhs[:, s, q, j, :], oh_hi[:, r, b, :],
                                                            start=False, stop=False)
                            last.then_inc(tile_done[l][r], 1)

                paired(pe, TURNS, edge_turn)
                if l == 1:
                    nc.tensor.matmul(cnt[:, 0:PQ], zero[:, 0:P], zero[:, 0:PQ], start=False, stop=True)
                for b in range(BANKS):
                    last = nc.tensor.matmul(acc[:, b, 0:HC], zero[:, 0:P], zero[:, :], start=False, stop=True)
                last.then_inc(acc_done[l], 1)
                pe.wait_ge(acc_copied[l], 1)
                for c in range(BLOCKS):
                    if c >= 2:
                        pe.wait_ge(sums_added[l], c - 1)
                    nc.tensor.transpose(ps_s[:, c % 2, 0:P], acc_sb[:, c * P:(c + 1) * P], ident[:, :]).then_inc(sums_turned[l], 1)


_INS = ["x", "src", "dst", "edge_attr_16", "edge_attr_2", "L0_gnn_weight", "L1_gnn_W_e", "L1_gnn_b_e", "L1_gnn_bias"]


def kernel(**inputs):
    import concourse.bacc as bacc
    from concourse.bass_utils import run_bass_kernel_spmd

    nc = bacc.Bacc("TRN2", target_bir_lowering=False, num_devices=1)
    arrays, args = {}, []
    for name in _INS:
        a = np.ascontiguousarray(inputs[name])
        arrays[f"in_{name}"] = a
        args.append(nc.dram_tensor(f"in_{name}", a.shape, mybir.dt.from_np(a.dtype), kind="ExternalInput").ap())
    out = nc.dram_tensor("out", (N_NODES, F), mybir.dt.float32, kind="ExternalOutput").ap()
    build(nc, *args, out)
    r = run_bass_kernel_spmd(nc, [arrays], core_ids=[0])
    return r.results[0]["out"]
```

```python
from contextlib import ExitStack

import concourse.bass as bass
import numpy as np
from concourse import mybir

P = 128
N_NODES, N_EDGES, F = 12500, 400000, 16
LO = P // F
BLOCKS = -(-N_NODES // (P * LO))
PADDED = BLOCKS * P * LO
WHOLE = N_NODES // (P * LO)
TAIL_P = (N_NODES - WHOLE * P * LO) // LO
TAIL_LO = N_NODES - WHOLE * P * LO - TAIL_P * LO
HI = -(-N_NODES // LO)
BANKS = 4
HC = -(-HI // BANKS)
TILES = N_EDGES // P
GT = 5
SLOTS = 5
TURN = GT * SLOTS
TURNS = TILES // TURN
PIECE = -(-TURNS // BLOCKS) * TURN
RING = 2 * GT
HI_DVE = [GT - 1, GT]
W = 32
GB = 4
K = 16
NB = 4
PARTS = 2
KF = K * F
ROW = [KF, KF + F]
EPS = 1e-5
SCALE = [2.0 ** 10, 2.0 ** 6]
M_LEAST, M_MOST = 2.0 ** -100, 2.0 ** 110
EXPONENT_BITS = 0x7F800000
PQ = BLOCKS * LO
FREE = 1


def build(nc, x_in, src_in, dst_in, ea16_in, ea2_in, w0_in, we_in, be_in, bias_in, out):
    fp32, bf16, fp16, i32 = mybir.dt.float32, mybir.dt.bfloat16, mybir.dt.float16, mybir.dt.int32
    ALU, ACT, AX = mybir.AluOpType, mybir.ActivationFunctionType, mybir.AxisListType
    MAX_ALL = bass.bass_isa.ReduceOp.max
    ds = bass.ds

    ctx = ExitStack()
    with ctx:
        def sb(name, shape, dt):
            return ctx.enter_context(nc.sbuf_tensor(name, shape, dt))

        def pb(name, shape, dt):
            return ctx.enter_context(nc.psum_tensor(name, shape, dt))

        def sem(name):
            return ctx.enter_context(nc.semaphore(name))

        table = [nc.dram_tensor(f"table{l}", (PADDED, ROW[l]), fp32, kind="Internal").ap() for l in (0, 1)]

        xs = sb("xs", [P, BLOCKS, P], fp32)
        hs = sb("hs", [P, BLOCKS, P], fp32)
        sq = sb("sq", [P, BLOCKS, P], fp32)
        stat = sb("stat", [P, 3, PQ], fp32)
        ends = [sb("dst_ids", [P, TILES], i32), sb("src_ids", [P, TILES], i32)]
        hi_all = sb("hi_all", [P, TILES], fp16)
        lo_all = sb("lo_all", [P, TILES], fp16)
        place_all = sb("place_all", [P, 2, TILES], fp16)
        near_all = place_all[:, 0, :]
        base_f = sb("base_f", [P, TURNS], fp32)
        base_i = sb("base_i", [1, TURNS], i32)
        reach = sb("reach", [P, 3], fp32)
        far = sb("far", [1, 2], i32)
        ones_row = sb("ones_row", [1, P], fp16)
        ident = sb("ident", [P, P], fp32)
        iota_hi = sb("iota_hi", [P, BANKS * HC], fp16)
        iota_lo = sb("iota_lo", [P, LO], fp16)
        iota_p = sb("iota_p", [P, P], fp32)
        iota_row = sb("iota_row", [P, P], fp32)
        minus_center = sb("minus_center", [P, NB], fp32)
        zero = sb("zero", [P, HC], fp16)
        one = sb("one", [P, 1], fp32)
        bias_rows = sb("bias_rows", [P, F], fp32)
        w_nat = sb("w_nat", [F, 2, K, F], fp32)
        w_row = sb("w_row", [F, 2, ROW[1]], fp32)
        w_bd = sb("w_bd", [P, LO, ROW[1]], fp32)
        largest = sb("largest", [P, 4], fp32)
        largest_all = sb("largest_all", [P, 4], fp32)
        ea_max = sb("ea_max", [P, TURNS], fp32)
        pow2 = sb("pow2", [P, 2], fp32)
        scale = sb("scale", [P, 2], fp32)
        h_blk = sb("h_blk", [P, 2, P], fp32)
        hT = sb("hT", [P, 2, P], fp32)
        ids = sb("ids", [P, 2, TURN], i32)
        g = sb("g", [P, SLOTS, GT, ROW[1]], fp32)
        g_flat = g[:, :, :, :].rearrange("p s t r -> p (s t r)")
        coef1 = sb("coef1", [P, SLOTS, GT, K], fp32)
        ea2 = sb("ea2", [P, TURN * 2], fp32)
        distance = sb("distance", [P, TURN, 2, NB], fp32)
        hats = sb("hats", [P, TURN, 2, NB], fp32)
        coef0 = sb("coef0", [P, 2, TURN, K], fp32)
        prod = sb("prod", [P, GT, F, K], fp32)
        msg = sb("msg", [P, 2, GT, F], fp32)
        part = sb("part", [P, PARTS, GT, F], fp16)
        hi_f = sb("hi_f", [P, SLOTS, GT], fp32)
        place_f = sb("place_f", [P, SLOTS, 2, GT], fp32)
        oh_lo = sb("oh_lo", [P, 2, TURN, LO], fp16)
        wide_lo = sb("wide_lo", [P, SLOTS, GT, P], fp16)
        lhs = sb("lhs", [P, SLOTS, PARTS, GT, P], fp16)
        hi_space = sb("hi_space", [P, RING * BANKS * HC], fp16)
        oh_hi = hi_space[:, :].rearrange("p (r b c) -> p r b c", b=BANKS, c=HC)
        oh_near = (hi_space[:, 0:2 * TURN * W]
                   .rearrange("p (a t w) -> p a t w", a=2, t=TURN))
        cnt_sb = hs[:, :, :].rearrange("p b c -> p (b c)")[0:LO, :]
        sq_hi = sb("sq_hi", [P, BANKS * HC], bf16)
        minus_hi = sb("minus_hi", [P, SLOTS, 1], fp32)
        sq_place = sb("sq_place", [P, RING, P + PQ], bf16)
        oh_place = sb("oh_place", [P, RING, P + PQ], bf16)
        acc_sb = sq[:, :, :].rearrange("p b c -> p (b c)")
        id_bits = (hi_space[:, :].bitcast(i32)[:, 0:2 * TILES]
                   .rearrange("p (a t) -> p a t", a=2))

        acc = pb("acc", [P, BANKS, 512], fp32)
        cnt = pb("cnt", [P, 512], fp32)
        ps_s = pb("ps_s", [P, 2, 512], fp32)

        x_loads, id_loads, bias_load = sem("x_loads"), sem("id_loads"), sem("bias_load")
        w_loads, w_rows, bd_zero = sem("w_loads"), sem("w_rows"), sem("bd_zero")
        iota_made, ident_made, consts_made, tail_zero = (
            sem("iota_made"), sem("ident_made"), sem("consts_made"), sem("tail_zero"))
        dve_step = sem("dve_step")
        act_step, ids_settled, blk_settled = sem("act_step"), sem("ids_settled"), sem("blk_settled")
        var_ready, sd_ready = sem("var_ready"), sem("sd_ready")
        largest_ready, largest_shared, scale_ready = sem("largest_ready"), sem("largest_shared"), sem("scale_ready")

        def by_layer(name):
            return [sem(f"{name}{l}") for l in (0, 1)]

        def by_slot(name, n):
            return [[sem(f"{name}{l}_{s}") for s in range(n)] for l in (0, 1)]

        bd_here, blk_ready, blk_turned, hT_ready, g_made = map(
            by_layer, ("bd_here", "blk_ready", "blk_turned", "hT_ready", "g_made"))
        g_copied, rows_stored = by_slot("g_copied", GB), by_slot("rows_stored", 2 * LO // GB)
        targets_ready, ids_ready, lo_ready, hi_staged, wide_ready, lhs_ready, hi_ready = map(
            by_layer, ("targets_ready", "ids_ready", "lo_ready", "hi_staged", "wide_ready", "lhs_ready", "hi_ready"))
        rows_here, rows_used = by_slot("rows_here", SLOTS), by_slot("rows_used", SLOTS)
        tile_done = by_slot("tile_done", RING)
        hi_negated, hi_squared, act_hi_ready = sem("hi_negated"), sem("hi_squared"), sem("act_hi_ready")
        coef_here = [sem(f"coef_here_{s}") for s in range(SLOTS)]
        ea_here, ea_used = sem("ea_here"), sem("ea_used")
        ea2_here, distance_made, hats_ready, coef0_made = sem("ea2_here"), sem("distance_made"), sem("hats_ready"), sem("coef0_made")
        base_spread, reach_ready, reach_turned, far_ready = (
            sem("base_spread"), sem("reach_ready"), sem("reach_turned"), sem("far_ready"))
        turn_step = by_layer("turn_step")
        window_settled, window_zero = sem("window_settled"), sem("window_zero")
        targets_split = by_layer("targets_split")
        places_step, places_ready = sem("places_step"), sem("places_ready")
        near_step, near_lhs, window_ready, window_added = sem("near_step"), sem("near_lhs"), sem("window_ready"), sem("window_added")
        place_staged, places_squared, cnt_ready = sem("place_staged"), sem("places_squared"), sem("cnt_ready")
        acc_done, acc_copied, sums_turned, sums_added = map(
            by_layer, ("acc_done", "acc_copied", "sums_turned", "sums_added"))
        x_final, stored = sem("x_final"), sem("stored")

        def paired(eng, n, body):
            with eng.Fori(0, n // 2) as k:
                body(k, 0)
                body(k, 1)
            body(n // 2, 0)

        def ring_slot(par, s, j):
            tile = par * TURN + s * GT + j
            return tile % RING, tile // RING

        ROUND = 2 * TURN // RING

        block = ctx.enter_context(nc.Block())
        top = WHOLE * P * LO

        @block.sync
        def _(sp):
            sp.wait_ge(tail_zero, 1)
            sp.dma_start(xs[:, 0:WHOLE, :], x_in[0:top, :].rearrange("(c p l) f -> p c (l f)", p=P, l=LO)).then_inc(x_loads, 16)
            sp.dma_start(xs[0:TAIL_P, WHOLE, :], x_in[top:top + TAIL_P * LO, :].rearrange("(p l) f -> p (l f)", l=LO)).then_inc(x_loads, 16)
            sp.dma_start(xs[TAIL_P:TAIL_P + 1, WHOLE, 0:TAIL_LO * F],
                         x_in[top + TAIL_P * LO:N_NODES, :].rearrange("(p l) f -> p (l f)", l=TAIL_LO)).then_inc(x_loads, 16)
            sp.dma_start(w_nat[:, 0, :, :], w0_in.rearrange("u v i o -> i (u v) o")).then_inc(w_loads, 16)
            sp.dma_start(w_nat[:, 1, :, :], we_in.rearrange("d (i o) -> i d o", o=F)).then_inc(w_loads, 16)
            sp.dma_start(w_row[:, 1, KF:KF + F], be_in.rearrange("(i o) -> i o", o=F)).then_inc(w_loads, 16)
            sp.dma_start(ends[1][:, :].rearrange("p (i t) -> p i t", t=TURN), src_in.rearrange("(i p t) -> p i t", p=P, t=TURN)).then_inc(id_loads, 16)
            sp.dma_start(ends[0][:, :].rearrange("p (i t) -> p i t", t=TURN), dst_in.rearrange("(i p t) -> p i t", p=P, t=TURN)).then_inc(id_loads, 16)
            sp.dma_start(bias_rows[:, :], bias_in.rearrange("(a o) -> a o", a=1).to_broadcast([P, F])).then_inc(bias_load, 16)
            ea = ea16_in.rearrange("(i p t) d -> i p (t d)", p=P, t=TURN)
            ea2_all = ea2_in.rearrange("(i p t) c -> i p (t c)", p=P, t=TURN)
            sp.wait_ge(w_rows, 1)
            sp.wait_ge(bd_zero, 1)
            for l in (0, 1):
                if l == 1:
                    sp.wait_ge(g_made[0], (BLOCKS + 2) * LO)
                for lo in range(LO):
                    sp.dma_start(w_bd[F * lo:F * lo + F, lo, 0:ROW[l]], w_row[:, l, 0:ROW[l]]).then_inc(bd_here[l], 16)
                if l == 1:
                    with sp.Fori(0, TURNS) as i:
                        sp.wait_ge(distance_made, FREE + i)
                        sp.dma_start(ea2[:, :], ea2_all[ds(i, 1), :, :].rearrange("a p c -> (a p) c")).then_inc(ea2_here, 16)
                        sp.wait_ge(ea_used, FREE + i)
                        sp.dma_start(coef1[:, :, :, :].rearrange("p s t d -> p (s t d)"),
                                     ea[ds(i, 1), :, :].rearrange("a p c -> (a p) c")).then_inc(ea_here, 16)
                    sp.wait_ge(ea_used, FREE + TURNS)
                rows = table[l].rearrange("(c p l) r -> c p (l r)", p=P, l=LO)

                def store_block(k, par):
                    c = k * 2 + par
                    for h in range(LO // GB):
                        for b in range(GB):
                            sp.wait_ge(g_copied[l][b], c * (LO // GB) + (h + 1 + FREE))
                        at, size = par * LO * ROW[1] + h * GB * ROW[l], GB * ROW[l]
                        sp.dma_start(rows[ds(c, 1), :, h * size:(h + 1) * size].rearrange("a p r -> (a p) r"),
                                     g_flat[:, at:at + size]).then_inc(rows_stored[l][par * (LO // GB) + h], 16)

                paired(sp, BLOCKS, store_block)
            with sp.Fori(0, TURNS) as i:
                for s in range(SLOTS):
                    sp.wait_ge(rows_used[1][s], FREE + i)
                    sp.dma_start(coef1[:, s, :, :].rearrange("p t d -> p (t d)"),
                                 ea[ds(i, 1), :, s * GT * K:(s + 1) * GT * K].rearrange("a p c -> (a p) c")).then_inc(coef_here[s], 16)
            sp.wait_ge(x_final, 1)
            sp.dma_start(out[0:top, :].rearrange("(c p l) f -> p c (l f)", p=P, l=LO), hs[:, 0:WHOLE, :]).then_inc(stored, 16)
            sp.dma_start(out[top:top + TAIL_P * LO, :].rearrange("(p l) f -> p (l f)", l=LO), hs[0:TAIL_P, WHOLE, :]).then_inc(stored, 16)
            sp.dma_start(out[top + TAIL_P * LO:N_NODES, :].rearrange("(p l) f -> p (l f)", l=TAIL_LO),
                         hs[TAIL_P:TAIL_P + 1, WHOLE, 0:TAIL_LO * F]).then_inc(stored, 16)
            sp.wait_ge(stored, 3 * 16)

        @block.gpsimd
        def _(pool):
            def iota(t, pattern, channel_multiplier):
                nc.gpsimd.iota(t, pattern, base=0, channel_multiplier=channel_multiplier,
                               allow_small_or_imprecise_dtypes=True).then_inc(iota_made, 1)

            iota(iota_p[:, :], [[1, P]], 0)
            iota(iota_row[:, :], [[0, P]], 1)
            iota(iota_lo[:, :], [[1, LO]], 0)
            iota(iota_hi[:, :], [[1, BANKS * HC]], 0)
            for l in (0, 1):
                pool.wait_ge(largest_ready, l + 1)
                nc.gpsimd.partition_all_reduce(largest_all[:, 3 * l:3 + l], largest[:, 3 * l:3 + l], P, MAX_ALL).then_inc(largest_shared, 1)
                pool.wait_ge(id_loads, 2 * 16)
                for slot in range(2 * LO // GB):
                    pool.wait_ge(rows_stored[l][slot], 16 * (FREE + (BLOCKS + 1 - slot // (LO // GB)) // 2))

                def gather_turn(k, par):
                    i = k * 2 + par
                    for s in range(SLOTS):
                        if s == 0:
                            pool.wait_ge(ids_ready[l], i + 1)
                        pool.wait_ge(rows_used[l][s], FREE + i)
                        pool.sem_inc(ids_settled, 1)
                        for j in range(GT):
                            nc.gpsimd.indirect_dma_start(
                                out=g[:, s, j, 0:ROW[l]], out_offset=None, in_=table[l],
                                in_offset=bass.IndirectOffsetOnAxis(ap=ids[:, par, s * GT + j:s * GT + j + 1], axis=0),
                            ).then_inc(rows_here[l][s], 16)

                paired(pool, TURNS, gather_turn)

        @block.scalar
        def _(act):
            def hat_functions(i):
                act.wait_ge(coef0_made, FREE + i)
                act.wait_ge(ea2_here, (i + 1) * 16)
                for u in range(NB):
                    a = nc.scalar.activation(distance[:, :, :, u].rearrange("p t a -> p (t a)"), ea2[:, :], ACT.Abs,
                                             bias=minus_center[:, u:u + 1])
                a.then_inc(distance_made, 1)
                act.wait_ge(distance_made, FREE + i + 1)
                nc.scalar.activation(hats[:, :, :, :], distance[:, :, :, :], ACT.Relu, bias=one[:, :],
                                     scale=-(NB - 1) / 2.0).then_inc(hats_ready, 1)

            act.wait_ge(consts_made, 1)
            act.sem_inc(distance_made, FREE)
            for l in (0, 1):
                for slot in range(2 * LO // GB):
                    act.sem_inc(rows_stored[l][slot], 16 * FREE)
                for b in range(GB):
                    act.sem_inc(g_copied[l][b], FREE)
                act.sem_inc(hT_ready[l], 2)
                act.wait_ge(var_ready, l + 1)
                nc.scalar.activation(stat[:, 2, :], stat[:, 1, :], ACT.Sqrt).then_inc(sd_ready, 1)
                act.wait_ge(scale_ready, l + 1)

                def take_block(c, par):
                    act.wait_ge(blk_turned[l], c + 3)
                    act.wait_ge(g_made[l], (c + 1) * LO)
                    nc.scalar.copy(hT[:, par, :], ps_s[:, par, 0:P]).then_inc(hT_ready[l], 1)

                def copy_rows(k, par):
                    c = k * 2 + par
                    for lo in range(0, LO, 2):
                        if lo % GB == 0:
                            act.wait_ge(rows_stored[l][par * (LO // GB) + lo // GB], (k + FREE) * 16)
                        act.wait_ge(g_made[l], c * LO + (2 * LO + lo + 1))
                        at = par * LO * ROW[1] + lo * ROW[l]
                        nc.scalar.activation(g_flat[:, at:at + ROW[l]], acc[:, lo % GB, 0:ROW[l]], ACT.Copy,
                                             scale=scale[:, l:l + 1]).then_inc(g_copied[l][lo % GB], 1)
                        if lo == 0 and not (isinstance(k, int) and c == BLOCKS - 1):
                            take_block(c + 1, 1 - par)

                act.wait_ge(id_loads, 2 * 16)
                if l == 1:
                    act.wait_ge(rows_used[0][SLOTS - 1], FREE + TURNS)
                nc.scalar.copy(ids[:, 0, :], ends[l][:, 0:TURN]).then_inc(ids_ready[l], 1)
                take_block(0, 0)
                paired(act, BLOCKS, copy_rows)
                act.wait_ge(targets_ready[l], (BLOCKS + FREE) * 2)

                def hand_ids(k, par):
                    i = k * 2 + par
                    if isinstance(k, int) and i == TURNS - 1:
                        return
                    act.wait_ge(rows_used[l][SLOTS - 1], FREE + i)
                    act.sem_inc(act_step, 1)
                    nc.scalar.copy(ids[:, 1 - par, :], ends[l][:, ds(i * TURN + TURN, TURN)]).then_inc(ids_ready[l], 1)

                def widen(par, s):
                    nc.scalar.copy(wide_lo[:, s, :, :].rearrange("p t (l f) -> p (t l) f", f=F),
                                   oh_lo[:, par, s * GT:(s + 1) * GT, :].rearrange("p t l -> p (t l)").unsqueeze(2)
                                   .to_broadcast([P, GT * LO, F])).then_inc(wide_ready[l], 1)

                def edge_turn(k, par):
                    i = k * 2 + par
                    act.wait_ge(lo_ready[l], i + 1)
                    for s in range(SLOTS):
                        act.wait_ge(hi_ready[l], (i * SLOTS + s + 1) * HI_DVE[l])
                        act.sem_inc(act_step, 1)
                        tiles = ds(i * TURN + s * GT, GT)
                        nc.scalar.copy(hi_f[:, s, :], hi_all[:, tiles]).then_inc(hi_staged[l], 1)
                        widen(par, s)
                        if l == 0:
                            nc.scalar.mul(minus_hi[:, s, :], hi_all[:, ds(i * TURN + (s * GT + GT - 1), 1)], -1.0).then_inc(hi_negated, 1)
                            act.wait_ge(hi_negated, i * SLOTS + s + 1)
                            nc.scalar.activation(sq_hi[:, :], iota_hi[:, :], ACT.Square, bias=minus_hi[:, s, :]).then_inc(hi_squared, 1)
                            act.wait_ge(hi_squared, i * SLOTS + s + 1)
                            r, before = ring_slot(par, s, GT - 1)
                            act.wait_ge(tile_done[0][r], k * ROUND + (FREE + before))
                            nc.scalar.activation(oh_hi[:, r, :, :].rearrange("p b c -> p (b c)"), sq_hi[:, :], ACT.Relu,
                                                 bias=one[:, :], scale=-1.0).then_inc(act_hi_ready, 1)
                        if s == 0:
                            hand_ids(k, par)
                        if l == 0 and s == 1 and not (isinstance(k, int) and i == TURNS - 1):
                            hat_functions(i + 1)
                        if l == 1:
                            nc.scalar.mul(place_f[:, s, :, :], place_all[:, :, tiles], -1.0).then_inc(place_staged, 1)
                            act.wait_ge(place_staged, i * SLOTS + s + 1)
                            for j in range(GT):
                                r, before = ring_slot(par, s, j)
                                act.wait_ge(tile_done[1][r], k * ROUND + (FREE + before))
                                nc.scalar.activation(sq_place[:, r, 0:P], iota_p[:, :], ACT.Square, bias=place_f[:, s, 0, j:j + 1])
                                nc.scalar.activation(sq_place[:, r, P:P + PQ], iota_p[:, 0:PQ], ACT.Square,
                                                     bias=place_f[:, s, 1, j:j + 1]).then_inc(places_squared, 1)
                                act.wait_ge(places_squared, i * TURN + s * GT + j + 1)
                                nc.scalar.activation(oh_place[:, r, :], sq_place[:, r, :], ACT.Relu, bias=one[:, :], scale=-1.0).then_inc(cnt_ready, 1)

                def near_turn(k, par):
                    i = k * 2 + par
                    act.wait_ge(lo_ready[1], i + 1)
                    for s in range(SLOTS):
                        act.wait_ge(near_lhs, i * SLOTS + s + 1)
                        widen(par, s)
                        if s == 0:
                            hand_ids(k, par)

                if l == 0:
                    hat_functions(0)
                    paired(act, TURNS, edge_turn)
                else:
                    act.wait_ge(far_ready, 1)
                    is_far = act.value_load(far[0:1, 0:1], min_val=0, max_val=1)
                    with act.If(is_far == 0):
                        paired(act, TURNS, near_turn)
                    with act.Else():
                        act.wait_ge(places_ready, 1)
                        paired(act, TURNS, edge_turn)

        @block.vector
        def _(dve):
            count = [0]

            def link(ins):
                count[0] += 1
                ins.then_inc(dve_step, 1)
                dve.wait_ge(dve_step, count[0])

            nc.vector.memset(xs[:, WHOLE, :], 0.0).then_inc(tail_zero, 1)
            nc.vector.memset(w_bd[:, :, :], 0.0).then_inc(bd_zero, 1)
            nc.vector.memset(zero[:, :], 0.0)
            for u in range(NB):
                nc.vector.memset(minus_center[:, u:u + 1], -float(np.linspace(-1.0, 1.0, NB, dtype=np.float32)[u]))
            nc.vector.memset(ones_row[:, :], 1.0)
            link(nc.vector.memset(one[:, :], 1.0))
            dve.sem_inc(consts_made, 1)
            dve.wait_ge(iota_made, 4)
            nc.vector.tensor_tensor(ident[:, :], iota_p[:, :], iota_row[:, :], ALU.is_equal).then_inc(ident_made, 1)
            dve.wait_ge(w_loads, 3 * 16)
            for l in (0, 1):
                last = nc.vector.tensor_copy(w_row[:, l, 0:KF].rearrange("i (o k) -> i o k", k=K),
                                             w_nat[:, l, :, :].rearrange("i k o -> i o k"))
            last.then_inc(w_rows, 1)
            link(nc.vector.memset(largest[:, :], 0.0))
            nc.vector.tensor_reduce(largest[0:F, 0:2], w_nat[:, :, :, :].rearrange("i l k o -> i l (k o)"), AX.X, ALU.max,
                                    apply_absolute_value=True)
            link(nc.vector.tensor_reduce(largest[0:F, 2:3], w_row[:, 1, KF:KF + F], AX.X, ALU.max, apply_absolute_value=True))
            dve.sem_inc(largest_ready, 1)
            dve.wait_ge(x_loads, 3 * 16)

            def node_view(t):
                return t[:, :, :].rearrange("p b (l f) -> p (b l) f", f=F)

            def over_features(i):
                return stat[:, i, :].unsqueeze(2).to_broadcast([P, PQ, F])

            dve.sem_inc(ea_used, FREE)
            dve.sem_inc(coef0_made, FREE)
            for l in (0, 1):
                for s in range(SLOTS):
                    dve.sem_inc(rows_used[l][s], FREE)
                dve.sem_inc(hi_ready[l], SLOTS * HI_DVE[l])
                link(nc.vector.tensor_reduce(stat[:, 0, :], node_view(xs), AX.X, ALU.add))
                link(nc.vector.tensor_scalar(stat[:, 0, :], stat[:, 0, :], 1.0 / F, None, ALU.mult))
                link(nc.vector.tensor_tensor(node_view(hs), node_view(xs), over_features(0), ALU.subtract))
                link(nc.vector.tensor_tensor(sq[:, :, :], hs[:, :, :], hs[:, :, :], ALU.mult))
                link(nc.vector.tensor_reduce(stat[:, 1, :], node_view(sq), AX.X, ALU.add))
                nc.vector.tensor_scalar(stat[:, 1, :], stat[:, 1, :], 1.0 / F, EPS, ALU.mult, ALU.add).then_inc(var_ready, 1)
                dve.wait_ge(sd_ready, l + 1)
                link(nc.vector.reciprocal(stat[:, 0, :], stat[:, 2, :]))
                link(nc.vector.tensor_tensor(node_view(hs), node_view(hs), over_features(0), ALU.mult))
                link(nc.vector.tensor_scalar(hs[:, :, :], hs[:, :, :], 0.0, None, ALU.max))
                dve.wait_ge(largest_shared, l + 1)
                big = largest_all[:, l:l + 1]
                if l == 1:
                    link(nc.vector.tensor_tensor(big, big, largest_all[:, 2:3], ALU.max))
                    link(nc.vector.tensor_scalar(largest_all[:, 3:4], largest_all[:, 3:4], 1.0, None, ALU.max))
                    link(nc.vector.tensor_tensor(big, big, largest_all[:, 3:4], ALU.mult))
                p2 = pow2[:, l:l + 1]
                link(nc.vector.tensor_scalar(p2, big, M_LEAST, M_MOST, ALU.max, ALU.min))
                link(nc.vector.tensor_scalar(p2.bitcast(i32), p2.bitcast(i32), EXPONENT_BITS, None, ALU.bitwise_and))
                link(nc.vector.tensor_scalar(p2, p2, 1.0 / SCALE[l], None, ALU.mult))
                link(nc.vector.reciprocal(scale[:, l:l + 1], p2))
                dve.sem_inc(scale_ready, 1)

                def hand_block(c, par):
                    dve.wait_ge(blk_turned[l], c + 1)
                    dve.sem_inc(blk_settled, 1)
                    nc.vector.tensor_copy(h_blk[:, par, :], hs[:, ds(c, 1), :].rearrange("p a c -> p (a c)")).then_inc(blk_ready[l], 1)

                def split_targets(c, first):
                    size = TILES - c * PIECE if isinstance(c, int) else PIECE
                    piece = ds(c * PIECE, size)
                    if first:
                        dve.wait_ge(targets_ready[l], (c + FREE) * 2)
                        nc.vector.tensor_scalar(id_bits[:, 0, 0:size], ends[1 - l][:, piece], 3, None, ALU.logical_shift_right).then_inc(targets_split[l], 1)
                        nc.vector.tensor_scalar(id_bits[:, 1, 0:size], ends[1 - l][:, piece], LO - 1, None, ALU.bitwise_and).then_inc(targets_split[l], 1)
                    else:
                        dve.wait_ge(targets_split[l], (c + 1) * 2)
                        nc.vector.tensor_copy(hi_all[:, piece], id_bits[:, 0, 0:size]).then_inc(targets_ready[l], 1)
                        nc.vector.tensor_copy(lo_all[:, piece], id_bits[:, 1, 0:size]).then_inc(targets_ready[l], 1)

                def copy_rows(k, par):
                    c = k * 2 + par
                    if not (isinstance(k, int) and c == BLOCKS - 1):
                        hand_block(c + 1, 1 - par)
                    for lo in range(1, LO, 2):
                        if lo % GB == 1:
                            dve.wait_ge(rows_stored[l][par * (LO // GB) + lo // GB], (k + FREE) * 16)
                        dve.wait_ge(g_made[l], c * LO + (2 * LO + lo + 1))
                        at = par * LO * ROW[1] + lo * ROW[l]
                        nc.vector.tensor_scalar(g_flat[:, at:at + ROW[l]], acc[:, lo % GB, 0:ROW[l]], scale[:, l:l + 1], None,
                                                ALU.mult).then_inc(g_copied[l][lo % GB], 1)
                        if lo in (1, GB + 1):
                            split_targets(c, lo == 1)

                dve.sem_inc(targets_ready[l], FREE * 2)
                if l == 0:
                    dve.wait_ge(id_loads, 2 * 16)
                hand_block(0, 0)
                paired(dve, BLOCKS, copy_rows)

                dve.wait_ge(targets_ready[l], (BLOCKS + FREE) * 2)
                to, bits = ends[1 - l][:, :], id_bits[:, 0, :]

                def find_windows():
                    dve.wait_ge(base_spread, 1)
                    link(nc.vector.tensor_copy(base_f[:, :], ps_s[:, 0, 0:TURNS]))
                    link(nc.vector.tensor_copy(base_i[:, :], base_f[0:1, :]))
                    link(nc.vector.tensor_tensor(near_all.rearrange("p (i t) -> p i t", t=TURN), hi_all[:, :].rearrange("p (i t) -> p i t", t=TURN),
                                                 base_f[:, :].unsqueeze(2).to_broadcast([P, TURNS, TURN]), ALU.subtract))
                    nc.vector.tensor_reduce(reach[:, 0:1], near_all, AX.X, ALU.max)
                    link(nc.vector.tensor_reduce(reach[:, 1:2], near_all, AX.X, ALU.min, negate=True))
                    link(nc.vector.tensor_scalar(reach[:, 0:1], reach[:, 0:1], -(W - 1.0), None, ALU.add))
                    link(nc.vector.tensor_tensor(reach[:, 2:3], reach[:, 0:1], reach[:, 1:2], ALU.max))
                    dve.sem_inc(reach_ready, 1)
                    dve.wait_ge(reach_turned, 1)
                    link(nc.vector.tensor_reduce(reach[0:1, 0:1], ps_s[0:1, 1, 0:P], AX.X, ALU.max))
                    link(nc.vector.tensor_scalar(far[:, 0:1], reach[0:1, 0:1], 0.0, None, ALU.is_gt))
                    dve.sem_inc(far_ready, 1)

                def find_places():
                    steps = [0]

                    def then(ins):
                        steps[0] += 1
                        ins.then_inc(places_step, 1)
                        dve.wait_ge(places_step, steps[0])

                    then(nc.vector.tensor_scalar(bits, to, 3, P - 1, ALU.logical_shift_right, ALU.bitwise_and))
                    then(nc.vector.tensor_copy(place_all[:, 0, :], bits))
                    then(nc.vector.tensor_scalar(bits, to, 10, 3, ALU.logical_shift_right, ALU.logical_shift_left))
                    then(nc.vector.tensor_tensor(place_all[:, 1, :], bits, lo_all[:, :], ALU.add))
                    dve.sem_inc(places_ready, 1)

                def prepare(i, par):
                    nc.vector.tensor_tensor(oh_lo[:, par, :, :], lo_all[:, ds(i * TURN, TURN)].unsqueeze(2).to_broadcast([P, TURN, LO]),
                                            iota_lo[:, :].unsqueeze(1).to_broadcast([P, TURN, LO]), ALU.is_equal).then_inc(lo_ready[l], 1)
                    if l == 0:
                        dve.wait_ge(ea_here, (i + 1) * 16)
                        nc.vector.tensor_reduce(ea_max[:, ds(i, 1)], coef1[:, :, :, :].rearrange("p s t d -> p (s t d)"),
                                                AX.X, ALU.max, apply_absolute_value=True).then_inc(ea_used, 1)
                        dve.wait_ge(hats_ready, i + 1)
                        nc.vector.tensor_tensor(coef0[:, par, :, :].rearrange("p t (u v) -> p t u v", v=NB),
                                                hats[:, :, 0, :].unsqueeze(3).to_broadcast([P, TURN, NB, NB]),
                                                hats[:, :, 1, :].unsqueeze(2).to_broadcast([P, TURN, NB, NB]), ALU.mult).then_inc(coef0_made, 1)

                STEPS = SLOTS * (4 + l)

                def left_operand(s, q):
                    return nc.vector.tensor_tensor(
                        lhs[:, s, q, :, :].rearrange("p t (l f) -> p t l f", f=F),
                        wide_lo[:, s, :, :].rearrange("p t (l f) -> p t l f", f=F),
                        part[:, q, :, :].unsqueeze(2).to_broadcast([P, GT, LO, F]), ALU.mult)

                def edge_turn(k, par):
                    i = k * 2 + par
                    is_last = isinstance(k, int) and i == TURNS - 1
                    at = [0]

                    def step(ins):
                        at[0] += 1
                        ins.then_inc(turn_step[l], 1)
                        return at[0]

                    def after(n):
                        dve.wait_ge(turn_step[l], i * STEPS + n)

                    for s in range(SLOTS):
                        def hi_onehot(j):
                            r, before = ring_slot(par, s, j)
                            dve.wait_ge(tile_done[l][r], k * ROUND + (FREE + before))
                            nc.vector.tensor_scalar(oh_hi[:, r, :, :].rearrange("p b c -> p (b c)"), iota_hi[:, :],
                                                    hi_f[:, s, j:j + 1], None, ALU.is_equal).then_inc(hi_ready[l], 1)

                        dve.wait_ge(rows_here[l][s], (i + 1) * (16 * GT))
                        if l == 0:
                            if s == 0:
                                dve.wait_ge(coef0_made, FREE + i + 1)
                            c = coef0[:, par, s * GT:(s + 1) * GT, :]
                        else:
                            dve.wait_ge(coef_here[s], (i + 1) * 16)
                            c = coef1[:, s, :, :]
                        m = msg[:, 0, :, :]
                        multiplied = step(nc.vector.tensor_tensor(prod[:, :, :, :], g[:, s, :, 0:KF].rearrange("p t (o k) -> p t o k", k=K),
                                                                  c.unsqueeze(2).to_broadcast([P, GT, F, K]), ALU.mult))
                        dve.wait_ge(hi_staged[l], i * SLOTS + (s + 1))
                        hi_onehot(0)
                        after(multiplied)
                        if l == 0:
                            dve.sem_inc(rows_used[l][s], 1)
                        summed = step(nc.vector.tensor_reduce(m, prod[:, :, :, :], AX.X, ALU.add))
                        hi_onehot(1)
                        after(summed)
                        if l == 1:
                            summed = step(nc.vector.tensor_tensor(m, m, g[:, s, :, KF:KF + F], ALU.add))
                            hi_onehot(2)
                            after(summed)
                            dve.sem_inc(rows_used[l][s], 1)
                        rounded = step(nc.vector.tensor_copy(part[:, 0, :, :], m))
                        hi_onehot(2 + l)
                        after(rounded)
                        rest = step(nc.vector.tensor_tensor(part[:, 1, :, :], m, part[:, 0, :, :], ALU.subtract))
                        dve.wait_ge(wide_ready[l], i * SLOTS + (s + 1))
                        left_operand(s, 0)
                        after(rest)
                        left_operand(s, 1).then_inc(lhs_ready[l], 1)
                        for j in range(3 + l, HI_DVE[l]):
                            hi_onehot(j)
                        if s == SLOTS - 2 and not is_last:
                            prepare(i + 1, 1 - par)
                    assert at[0] == STEPS

                def near_onehot(i, par):
                    nc.vector.tensor_tensor(oh_near[:, par, :, :], near_all[:, ds(i * TURN, TURN)].unsqueeze(2).to_broadcast([P, TURN, W]),
                                            iota_hi[:, 0:W].unsqueeze(1).to_broadcast([P, TURN, W]), ALU.is_equal)

                def near_turn(k, par):
                    i = k * 2 + par
                    at = [0]

                    def then(ins):
                        at[0] += 1
                        ins.then_inc(near_step, 1)
                        dve.wait_ge(near_step, i * (SLOTS * 5) + at[0])

                    for s in range(SLOTS):
                        dve.wait_ge(rows_here[1][s], (i + 1) * (16 * GT))
                        dve.wait_ge(coef_here[s], (i + 1) * 16)
                        m = msg[:, 0, :, :]
                        then(nc.vector.tensor_tensor(prod[:, :, :, :], g[:, s, :, 0:KF].rearrange("p t (o k) -> p t o k", k=K),
                                                     coef1[:, s, :, :].unsqueeze(2).to_broadcast([P, GT, F, K]), ALU.mult))
                        then(nc.vector.tensor_reduce(m, prod[:, :, :, :], AX.X, ALU.add))
                        then(nc.vector.tensor_tensor(m, m, g[:, s, :, KF:KF + F], ALU.add))
                        dve.sem_inc(rows_used[1][s], 1)
                        then(nc.vector.tensor_copy(part[:, 0, :, :], m))
                        rest = nc.vector.tensor_tensor(part[:, 1, :, :], m, part[:, 0, :, :], ALU.subtract)
                        at[0] += 1
                        rest.then_inc(near_step, 1)
                        dve.wait_ge(wide_ready[1], i * SLOTS + (s + 1))
                        left_operand(s, 0)
                        dve.wait_ge(near_step, i * (SLOTS * 5) + at[0])
                        left_operand(s, 1).then_inc(near_lhs, 1)
                        if s == SLOTS - 2 and not (isinstance(k, int) and i == TURNS - 1):
                            near_onehot(i + 1, 1 - par)
                            prepare(i + 1, 1 - par)
                    at_hi = dve.value_load(base_i[0:1, ds(i, 1)], min_val=0, max_val=HI)
                    dve.wait_ge(window_ready, i + 1)
                    dve.sem_inc(window_settled, 1)
                    place = acc_sb[:, ds(at_hi, W)]
                    nc.vector.tensor_tensor(place, place, acc[:, par, 0:W], ALU.add).then_inc(window_added, 1)
                    place = cnt_sb[:, ds(at_hi, W)]
                    nc.vector.tensor_tensor(place, place, acc[0:LO, 2 + par, 0:W], ALU.add).then_inc(window_added, 1)
                    dve.wait_ge(window_added, (i + 1) * 2)

                def all_turns():
                    prepare(0, 0)
                    paired(dve, TURNS, edge_turn)
                    dve.wait_ge(acc_done[l], 1)
                    nc.vector.memset(acc_sb[:, BANKS * HC:], 0.0)
                    nc.vector.tensor_copy(acc_sb[:, 0:BANKS * HC].rearrange("p (b c) -> p b c", b=BANKS),
                                          acc[:, :, 0:HC]).then_inc(acc_copied[l], 1)

                if l == 0:
                    all_turns()
                    link(nc.vector.tensor_reduce(largest[:, 3:4], ea_max[:, :], AX.X, ALU.max))
                    dve.sem_inc(largest_ready, 1)
                else:
                    find_windows()
                    is_far = dve.value_load(far[0:1, 0:1], min_val=0, max_val=1)
                    with dve.If(is_far == 0):
                        dve.sem_inc(near_lhs, SLOTS)
                        nc.vector.memset(cnt_sb[:, :], 0.0)
                        nc.vector.memset(acc_sb[:, :], 0.0).then_inc(window_zero, 1)
                        near_onehot(0, 0)
                        prepare(0, 0)
                        dve.wait_ge(window_zero, 1)
                        paired(dve, TURNS, near_turn)
                        dve.sem_inc(acc_copied[1], 1)
                        dve.wait_ge(acc_done[1], 1)
                    with dve.Else():
                        find_places()
                        all_turns()
                if l == 1:
                    link(nc.vector.tensor_scalar(stat[:, 0, :], cnt[:, 0:PQ], 1.0, None, ALU.max))
                    link(nc.vector.reciprocal(stat[:, 1, :], stat[:, 0, :]))
                for c in range(BLOCKS):
                    dve.wait_ge(sums_turned[l], c + 1)
                    src = ps_s[:, c % 2, 0:P]
                    if l == 0:
                        nc.vector.scalar_tensor_tensor(out=xs[:, c, :], in0=src, scalar=pow2[:, 0:1], in1=xs[:, c, :],
                                                       op0=ALU.mult, op1=ALU.add).then_inc(sums_added[l], 1)
                    else:
                        nc.vector.tensor_scalar(hs[:, c, :], src, pow2[:, 1:2], None, ALU.mult).then_inc(sums_added[l], 1)
                dve.wait_ge(sums_added[l], BLOCKS)
            dve.wait_ge(bias_load, 16)
            link(nc.vector.tensor_tensor(node_view(hs), node_view(hs), over_features(1), ALU.mult))
            link(nc.vector.tensor_tensor(node_view(hs), node_view(hs), bias_rows[:, :].unsqueeze(1).to_broadcast([P, PQ, F]), ALU.add))
            nc.vector.tensor_tensor(hs[:, :, :], hs[:, :, :], xs[:, :, :], ALU.add).then_inc(x_final, 1)

        @block.tensor
        def _(pe):
            pe.wait_ge(ident_made, 1)
            pe.wait_ge(consts_made, 1)
            for l in (0, 1):
                pe.sem_inc(blk_turned[l], 2)
                pe.sem_inc(g_made[l], 2 * LO)
                for r in range(RING):
                    pe.sem_inc(tile_done[l][r], FREE)
                pe.wait_ge(bd_here[l], LO * 16)

                def turn_block(c, par):
                    pe.wait_ge(blk_ready[l], c + 1)
                    pe.wait_ge(hT_ready[l], c + 1)
                    nc.tensor.transpose(ps_s[:, par, 0:P], h_blk[:, par, :], ident[:, :]).then_inc(blk_turned[l], 1)

                def make_rows(k, par):
                    c = k * 2 + par
                    if not (isinstance(k, int) and c == BLOCKS - 1):
                        turn_block(c + 1, 1 - par)
                    pe.wait_ge(hT_ready[l], c + 3)
                    for lo in range(LO):
                        pe.wait_ge(g_copied[l][lo % GB], c * (LO // GB) + (FREE + lo // GB))
                        nc.tensor.matmul(acc[:, lo % GB, 0:ROW[l]], hT[:, par, :], w_bd[:, lo, 0:ROW[l]],
                                         start=True, stop=True).then_inc(g_made[l], 1)

                turn_block(0, 0)
                paired(pe, BLOCKS, make_rows)
                for b in range(GB):
                    pe.wait_ge(g_copied[l][b], BLOCKS * (LO // GB) + FREE)

                def edge_turn(k, par):
                    i = k * 2 + par
                    for s in range(SLOTS):
                        pe.wait_ge(lhs_ready[l], i * SLOTS + s + 1)
                        for j in range(GT):
                            r, _ = ring_slot(par, s, j)
                            if j < HI_DVE[l]:
                                pe.wait_ge(hi_ready[l], (i * SLOTS + (SLOTS + s)) * HI_DVE[l] + (j + 1))
                            else:
                                pe.wait_ge(act_hi_ready, i * SLOTS + s + 1)
                            if l == 1:
                                pe.wait_ge(cnt_ready, i * TURN + s * GT + j + 1)
                                nc.tensor.matmul(cnt[:, 0:PQ], oh_place[:, r, 0:P], oh_place[:, r, P:P + PQ], start=False, stop=False)
                            for q in range(PARTS):
                                for b in range(BANKS):
                                    last = nc.tensor.matmul(acc[:, b, 0:HC], lhs[:, s, q, j, :], oh_hi[:, r, b, :],
                                                            start=False, stop=False)
                            last.then_inc(tile_done[l][r], 1)

                def all_turns():
                    for b in range(BANKS):
                        nc.tensor.matmul(acc[:, b, 0:HC], zero[:, 0:P], zero[:, :], start=True, stop=False)
                    if l == 1:
                        nc.tensor.matmul(cnt[:, 0:PQ], zero[:, 0:P], zero[:, 0:PQ], start=True, stop=False)
                    paired(pe, TURNS, edge_turn)
                    if l == 1:
                        nc.tensor.matmul(cnt[:, 0:PQ], zero[:, 0:P], zero[:, 0:PQ], start=False, stop=True)
                    for b in range(BANKS):
                        last = nc.tensor.matmul(acc[:, b, 0:HC], zero[:, 0:P], zero[:, :], start=False, stop=True)
                    last.then_inc(acc_done[l], 1)
                    pe.wait_ge(acc_copied[l], 1)

                def near_turn(k, par):
                    i = k * 2 + par
                    for s in range(SLOTS):
                        pe.wait_ge(near_lhs, i * SLOTS + (SLOTS + s + 1))
                        for j in range(GT):
                            t = s * GT + j
                            for q in range(PARTS):
                                nc.tensor.matmul(acc[:, par, 0:W], lhs[:, s, q, j, :], oh_near[:, par, t, :],
                                                 start=(t == 0 and q == 0), stop=(t == TURN - 1 and q == PARTS - 1))
                            last = nc.tensor.matmul(acc[0:LO, 2 + par, 0:W], oh_lo[:, par, t, :], oh_near[:, par, t, :],
                                                    start=(t == 0), stop=(t == TURN - 1))
                    last.then_inc(window_ready, 1)

                if l == 0:
                    all_turns()
                else:
                    pe.wait_ge(targets_ready[1], (BLOCKS + FREE) * 2)
                    nc.tensor.matmul(ps_s[:, 0, 0:TURNS], ones_row[:, :], hi_all[0:1, :].rearrange("a (i t) -> a i t", t=TURN)[:, :, 0],
                                     start=True, stop=True).then_inc(base_spread, 1)
                    pe.wait_ge(reach_ready, 1)
                    nc.tensor.transpose(ps_s[0:1, 1, 0:P], reach[:, 2:3], ident[:, :]).then_inc(reach_turned, 1)
                    pe.wait_ge(far_ready, 1)
                    is_far = pe.value_load(far[0:1, 0:1], min_val=0, max_val=1)
                    with pe.If(is_far == 0):
                        paired(pe, TURNS, near_turn)
                        pe.wait_ge(acc_copied[1], 1)
                        for c in range(BLOCKS):
                            last = nc.tensor.transpose(cnt[:, c * LO:(c + 1) * LO], cnt_sb[:, c * P:(c + 1) * P], ident[0:LO, 0:LO])
                        last.then_inc(acc_done[1], 1)
                    with pe.Else():
                        all_turns()
                for c in range(BLOCKS):
                    if c >= 2:
                        pe.wait_ge(sums_added[l], c - 1)
                    nc.tensor.transpose(ps_s[:, c % 2, 0:P], acc_sb[:, c * P:(c + 1) * P], ident[:, :]).then_inc(sums_turned[l], 1)


_INS = ["x", "src", "dst", "edge_attr_16", "edge_attr_2", "L0_gnn_weight", "L1_gnn_W_e", "L1_gnn_b_e", "L1_gnn_bias"]


def kernel(**inputs):
    import concourse.bacc as bacc
    from concourse.bass_utils import run_bass_kernel_spmd

    nc = bacc.Bacc("TRN2", target_bir_lowering=False, num_devices=1)
    arrays, args = {}, []
    for name in _INS:
        a = np.ascontiguousarray(inputs[name])
        arrays[f"in_{name}"] = a
        args.append(nc.dram_tensor(f"in_{name}", a.shape, mybir.dt.from_np(a.dtype), kind="ExternalInput").ap())
    out = nc.dram_tensor("out", (N_NODES, F), mybir.dt.float32, kind="ExternalOutput").ap()
    build(nc, *args, out)
    r = run_bass_kernel_spmd(nc, [arrays], core_ids=[0])
    return r.results[0]["out"]
```
